# Optimizing a Trainium2 kernel written in Bass

```python
import numpy as np
import jax
import jax.numpy as jnp

def _softmax(x, axis=-1):
    return jax.nn.softmax(x, axis=axis)

def _gelu(x):
    return jax.nn.gelu(x, approximate=True)

def _silu(x):
    return jax.nn.silu(x)

def _sigmoid(x):
    return jax.nn.sigmoid(x)

def _layernorm(x, axis=-1, eps=1e-05):
    m = jnp.mean(x, axis=axis, keepdims=True)
    v = jnp.var(x, axis=axis, keepdims=True)
    return (x - m) / jnp.sqrt(v + eps)

def _scatter_add(tgt, idx, src, axis=0):
    return tgt.at[idx].add(src)

def _segment_sum(src, seg, n):
    return jax.ops.segment_sum(src, seg, n)
kernel_name = 'mk_metaformer_d1_conv_nhwc128_r4_91893a'

def setup_inputs(seed: int=0):
    np.random.seed(seed)
    _w = jnp.asarray

    def _rec_inputs():
        import jax
        import jax.numpy as jnp
        _gk = jax.random.key(seed)
        x = -7.109e-05 + 0.9999 * jax.random.normal(jax.random.fold_in(_gk, 1), (32, 32, 32, 32), jnp.float32)
        return x
    x = _rec_inputs()

    def _L0_conv_setup():
        import jax, jax.numpy as jnp
        import numpy as np
        B, H, W, C = (32, 32, 32, 32)
        key = jax.random.key(seed)
        k1, k2 = jax.random.split(key)
        x = jax.random.normal(k1, (B, H, W, C), dtype=jnp.float32)
        W_sel = jax.random.normal(k2, (C, 4), dtype=jnp.float32) * 0.05
        b_sel = jnp.zeros((4,), dtype=jnp.float32)
        return {'x': x, 'W_sel': W_sel, 'b_sel': b_sel}
    _L0_conv_all = _L0_conv_setup()
    _L0_conv_in = {k: v for k, v in _L0_conv_all.items() if k in ('W_sel', 'b_sel')}
    del _L0_conv_all

    def _L0_ffn_setup():
        import jax, jax.numpy as jnp
        import numpy as np
        B, S, D, E, H, O, K = (128, 512, 32, 16, 128, 32, 8)
        key = jax.random.key(seed)
        k0, k1, k2, k3 = jax.random.split(key, 4)
        x = jax.random.normal(k0, (B, S, D), dtype=jnp.float32)
        gate_w = jax.random.normal(k1, (E, D), dtype=jnp.float32) * (1.0 / np.sqrt(D))
        gate_b = jnp.zeros((E,), dtype=jnp.float32)
        weight1 = jax.random.uniform(k2, (E, D + 1, H), dtype=jnp.float32, minval=-1.0, maxval=1.0) * (1.0 / np.sqrt(D + 1))
        weight2 = jax.random.uniform(k3, (E, H + 1, O), dtype=jnp.float32, minval=-1.0, maxval=1.0) * (1.0 / np.sqrt(H + 1))
        return {'x': x, 'gate_w': gate_w, 'gate_b': gate_b, 'weight1': weight1, 'weight2': weight2}
    _L0_ffn_all = _L0_ffn_setup()
    _L0_ffn_in = {k: v for k, v in _L0_ffn_all.items() if k in ('gate_w', 'gate_b', 'weight1', 'weight2')}
    del _L0_ffn_all
    return {'x': x, 'L0_conv_W_sel': _L0_conv_in['W_sel'], 'L0_conv_b_sel': _L0_conv_in['b_sel'], 'L0_ffn_gate_w': _L0_ffn_in['gate_w'], 'L0_ffn_gate_b': _L0_ffn_in['gate_b'], 'L0_ffn_weight1': _L0_ffn_in['weight1'], 'L0_ffn_weight2': _L0_ffn_in['weight2']}

def reference(x, L0_conv_W_sel, L0_conv_b_sel, L0_ffn_gate_w, L0_ffn_gate_b, L0_ffn_weight1, L0_ffn_weight2):
    import jax
    import jax.numpy as jnp

    def _L0_conv_ref(x, W_sel, b_sel):
        import jax, jax.numpy as jnp
        import numpy as np
        B, H, W, C = (32, 32, 32, 32)
        pooled = jnp.mean(x, axis=(1, 2))
        weights = jax.nn.softmax(pooled @ W_sel + b_sel, axis=-1)
        out = jnp.zeros_like(x)
        for i in range(4):
            rot = jnp.rot90(x, k=i, axes=(1, 2))
            out = out + rot * weights[:, i, None, None, None]
        return out

    def _L0_ffn_ref(x, gate_w, gate_b, weight1, weight2):
        import jax, jax.numpy as jnp
        import numpy as np
        B, S, D, E, H, O, K = (128, 512, 32, 16, 128, 32, 8)
        Bn, Sn, Dn = x.shape
        logits = jnp.einsum('bsd,ed->bse', x, gate_w) + gate_b
        probs = jax.nn.softmax(logits, axis=1)
        vals, idx = jax.lax.top_k(probs.transpose(0, 2, 1), K)
        topv = vals.transpose(0, 2, 1)
        topi = idx.transpose(0, 2, 1)
        flat_idx = topi.reshape(Bn, K * E)
        gathered = jnp.take_along_axis(x, flat_idx[:, :, None], axis=1)
        gathered = gathered.reshape(Bn, K, E, Dn)
        pooled = jnp.einsum('bked,bke->bed', gathered, topv)
        ones = jnp.ones((E, Bn, 1), dtype=x.dtype)
        h = jnp.concatenate([pooled.transpose(1, 0, 2), ones], axis=-1)
        h = jax.nn.gelu(jnp.einsum('ebd,edh->ebh', h, weight1), approximate=False)
        h = jnp.concatenate([h, ones], axis=-1)
        out = jnp.einsum('ebh,eho->ebo', h, weight2)
        out = out.transpose(1, 0, 2)
        weighted = jnp.einsum('beo,bke->bkeo', out, topv).reshape(Bn, K * E, O)
        outputs = jnp.zeros((Bn, Sn, O), dtype=x.dtype)
        outputs = outputs.at[jnp.arange(Bn)[:, None], flat_idx].add(weighted)
        return outputs

    def _gn(v, G=32, eps=1e-05):
        B_, H_, W_, C_ = v.shape
        g = v.reshape(B_, H_, W_, G, C_ // G)
        m = jnp.mean(g, axis=(1, 2, 4), keepdims=True)
        s = jnp.var(g, axis=(1, 2, 4), keepdims=True)
        return ((g - m) / jnp.sqrt(s + eps)).reshape(v.shape)

    def _ln_c(v, eps=1e-06):
        m = jnp.mean(v, axis=-1, keepdims=True)
        s = jnp.var(v, axis=-1, keepdims=True)
        return (v - m) / jnp.sqrt(s + eps)

    def _ln_t(v, eps=1e-05):
        m = jnp.mean(v, axis=-1, keepdims=True)
        s = jnp.var(v, axis=-1, keepdims=True)
        return (v - m) / jnp.sqrt(s + eps)

    def _to_tokens(v):
        B_, H_, W_, C_ = v.shape
        return v.reshape(B_, H_ * W_, C_)

    def _from_tokens(t, like):
        return t.reshape(like.shape)
    x = x + _L0_conv_ref(_ln_c(x), L0_conv_W_sel, L0_conv_b_sel)
    t = _to_tokens(x)
    t = t + _L0_ffn_ref(_ln_t(t), L0_ffn_gate_w, L0_ffn_gate_b, L0_ffn_weight1, L0_ffn_weight2)
    x = _from_tokens(t, x)
    return x

_drawn_inputs = setup_inputs


def setup_inputs(seed=0):
    import zlib

    import numpy as np

    out = dict(_drawn_inputs(seed))
    spreads = {'L0_conv_b_sel': (0.0, 0.1), 'L0_ffn_gate_b': (0.0, 0.1)}
    factors = {'L0_conv_W_sel': 8.0, 'L0_ffn_gate_w': 8.0, 'L0_ffn_weight1': 8.0, 'L0_ffn_weight2': 8.0}
    for name, (base, spread) in spreads.items():
        noise = np.random.default_rng([zlib.crc32(name.encode()), seed]).standard_normal(out[name].shape)
        drawn = base * np.exp(spread * noise) if base else spread * noise
        out[name] = jnp.asarray(drawn.astype(out[name].dtype))
    for name, factor in factors.items():
        out[name] = (out[name] * factor).astype(out[name].dtype)
    return out
```

```python
from contextlib import ExitStack

import concourse.bass as bass
from concourse import mybir

ALU = mybir.AluOpType
ACT = mybir.ActivationFunctionType
AX = mybir.AxisListType
F32 = mybir.dt.float32

P = 128
BANK = 512
TOPK = 8
ROTS = 4
EPS_IN = 1e-6
EPS_TOK = 1e-5


class Links:

    def __init__(self, eng, sem, per):
        self.eng, self.sem, self.per = eng, sem, per

    def begin(self, n):
        self.base, self.i = n * self.per, 0

    def then(self, ins):
        self.i += 1
        ins.then_inc(self.sem, 1)
        self.eng.wait_ge(self.sem, self.base + self.i)

    def end(self):
        assert self.i == self.per, (self.i, self.per)


def reach(eng, sem, value):
    if value > 0:
        eng.wait_ge(sem, value)


def rotate_and_route_kernel(
    nc: bass.Bass,
    x: bass.AP,
    W_sel: bass.AP,
    b_sel: bass.AP,
    gate_w: bass.AP,
    gate_b: bass.AP,
    weight1: bass.AP,
    weight2: bass.AP,
    out: bass.AP,
):
    B, HH, WW, C = x.shape
    E, _, H = weight1.shape
    O = weight2.shape[2]
    S = HH * WW
    GB = P // C
    NG = B // GB
    NP = NG // 2
    SH = S // BANK
    J = BANK // P
    GT = GB * SH * J
    PB = 2 * GB
    LC = GB * E + GB
    assert (HH, WW, C, E, H, O) == (32, 32, 32, 16, 128, 32) and PB * E == P and NG % 2 == 0

    with ExitStack() as ctx:
        def sb(name, shape):
            return ctx.enter_context(nc.sbuf_tensor(name, shape, F32))

        def sem(name):
            return ctx.enter_context(nc.semaphore(name))

        psum = ctx.enter_context(nc.psum_tensor("psum", [P, 8, BANK], F32))
        TURN, CONV, LOGI, ROWS = 0, 2, 4, 6

        ident = sb("ident", [P, P])
        same_image = sb("same_image", [P, P])
        own_slot = sb("own_slot", [P, PB, O])
        gate_rows = sb("gate_rows", [GB * E, C])
        gate_sum = sb("gate_sum", [GB * E, 1])
        gate_avg = sb("gate_avg", [GB * E, 1])
        gate_diag = sb("gate_diag", [GB * E, GB, C])
        gate_cent = sb("gate_cent", [GB * E, C])
        gate_mean = sb("gate_mean", [P, LC])
        wsel = sb("wsel", [P, ROTS])
        bsel = sb("bsel", [P, ROTS])
        gateb = sb("gateb", [P, 1])
        w1 = sb("w1", [C + 1, E, H])
        w2 = sb("w2", [H, E, O])
        b2_rows = sb("b2_rows", [E, O])
        b2 = sb("b2", [O, E])

        x_in = sb("x_in", [P, 2, GB, SH, J * C])
        x_cols = sb("x_cols", [P, 2, SH * J, GB, C])
        y_tok = sb("y_tok", [P, 2, SH * J, GB, C])
        y_chan = sb("y_chan", [P, 2, S])
        x1_chan = sb("x1_chan", [P, 2, SH, J, P])
        sum1 = sb("sum1", [P, GT])
        mean1 = sb("mean1", [P, 2, GT])
        square1 = sb("square1", [P, GT * C])
        ssum1 = sb("ssum1", [P, GT])
        var1 = sb("var1", [P, GT])
        ln1 = sb("ln1", [P, GT])
        r1 = sb("r1", [P, GT])
        n1 = sb("n1", [P, 2, GT])
        rstd1 = sb("rstd1", [P, GT])
        chan_sum = sb("chan_sum", [P, 2, SH])
        pooled = sb("pooled", [P, 1])
        wsel_rhs = sb("wsel_rhs", [P, ROTS])
        rot_logit = sb("rot_logit", [P, ROTS])
        rot_nmax = sb("rot_nmax", [P, 1])
        rot_exp = sb("rot_exp", [P, ROTS])
        rot_den = sb("rot_den", [P, 1])
        rot_rden = sb("rot_rden", [P, 1])
        rot_w = sb("rot_w", [P, 2, ROTS])
        diag = sb("diag", [P, 2, P])
        square2 = sb("square2", [P, GB, SH, J, C])
        ssum2 = sb("ssum2", [P, GT])
        mean2 = sb("mean2", [P, GB, SH, J])
        msq2 = sb("msq2", [P, GT])
        vraw2 = sb("vraw2", [P, GT])
        var2 = sb("var2", [P, GT])
        ln2 = sb("ln2", [P, GT])
        r2 = sb("r2", [P, GT])
        n2 = sb("n2", [P, 2, GT])

        rstd2 = sb("rstd2", [P, 2, GB, SH, J])
        logit_tok = sb("logit_tok", [P, SH * J, 2, GB, E])
        top = sb("top", [P, TOPK])
        top_e = sb("top_e", [P, TOPK])
        gb_max = sb("gb_max", [P, 1])
        neg_max = sb("neg_max", [P, 1])
        den = sb("den", [P, 1])
        rden = sb("rden", [P, 1])
        prob = sb("prob", [P, S])
        rest = sb("rest", [P, S])
        picked = sb("picked", [P, S])
        take = sb("take", [P, S])
        take_tok = sb("take_tok", [P, SH * J, PB, E])
        slot_sum = sb("slot_sum", [E, PB])
        slot_mean = sb("slot_mean", [E, PB])

        x1 = sb("x1", [P, B, SH, J, C])
        take_all = sb("take_all", [P, NP, S])
        slots = sb("slots", [E, B, C])
        slots_c = sb("slots_c", [C + 1, B, E])
        hidden = sb("hidden", [H, E, B])
        slot_out = sb("slot_out", [O, B, E])
        spread = sb("spread", [P, NP, PB, O])

        x_loaded = [sem("x_loaded_even"), sem("x_loaded_odd")]
        c_loaded = sem("constants_loaded")
        w_loaded = sem("expert_weights_loaded")
        mask_link = sem("mask_link")
        masks = sem("masks_made")
        gate_set = sem("gate_set")
        gate_link = sem("gate_link")
        gate_diag_ready = sem("gate_diag_ready")
        gate_turned = sem("gate_turned")
        gate_ready = sem("gate_ready")
        mean1_link = sem("mean1_link")
        mean1_ready = sem("mean1_ready")
        centred = sem("centred")
        square1_ready = sem("square1_ready")
        square1_used = sem("square1_used")
        var1_ready = sem("var1_ready")
        ln1_link = sem("ln1_link")
        r1_ready = sem("r1_ready")
        norm1_link = sem("norm1_link")
        y_ready = sem("y_ready")
        y_turned = sem("y_turned")
        x_ordered = sem("x_ordered")
        x_turned = sem("x_turned")
        y_chan_ready = sem("y_chan_ready")
        pool_link = sem("pool_link")
        wsel_rhs_ready = sem("wsel_rhs_ready")
        rot_logits = sem("rot_logits")
        rot_link = sem("rot_link")
        rot_nmax_ready = sem("rot_nmax_ready")
        rot_exp_ready = sem("rot_exp_ready")
        rot_w_link = sem("rot_w_link")
        diag_ready = sem("diag_ready")
        conv_done = sem("conv_done")
        conv_used = sem("conv_used")
        x1_ready = sem("x1_ready")
        x1_turned = sem("x1_turned")
        square2_ready = sem("square2_ready")
        square2_used = sem("square2_used")
        x1_kept = sem("x1_kept")
        logits_done = sem("logits_done")
        stat2_link = sem("stat2_link")
        var2_ready = sem("var2_ready")
        ln2_link = sem("ln2_link")
        r2_ready = sem("r2_ready")
        norm2_link = sem("norm2_link")
        logit_ready = sem("logit_ready")
        rows_done = sem("rows_done")
        max_link = sem("max_link")
        neg_max_ready = sem("neg_max_ready")
        prob_ready = sem("prob_ready")
        rest_ready = sem("rest_ready")
        picked_ready = sem("picked_ready")
        take_ready = sem("take_ready")
        take_turned = sem("take_turned")
        take_kept = sem("take_kept")
        take_tok_ready = sem("take_tok_ready")
        gathered = sem("gathered")
        gather_link = sem("gather_link")
        slots_ready = sem("slots_ready")
        slots_turned = sem("slots_turned")
        slots_c_ready = sem("slots_c_ready")
        hidden_done = sem("hidden_done")
        hidden_ready = sem("hidden_ready")
        slot_out_done = sem("slot_out_done")
        slot_out_ready = sem("slot_out_ready")
        slot_out_turned = sem("slot_out_turned")
        spread_ready = sem("spread_ready")
        scattered = sem("scattered")
        added = sem("added")
        stored = sem("stored")

        x_dram = x.rearrange("(g b) h w c -> g b (h w) c", b=GB).rearrange(
            "g b (s p j) c -> g p b s (j c)", p=P, j=J)
        out_dram = out.rearrange("b h w c -> b (h w) c").rearrange(
            "b (s p j) c -> p b s (j c)", p=P, j=J)

        def token_groups(t):
            return t.rearrange("p b s (j c) -> p (b s j) c", c=C)

        def spread_over(stat, n):
            return stat.unsqueeze(2).broadcast_to([P, stat.shape[1], n])

        HIDDEN_BANKS = [CONV, CONV + 1, ROWS, ROWS + 1]
        OUT_BANK = LOGI + 1

        block = ctx.enter_context(nc.Block())

        def is_group(g):
            return 0 <= g < NG

        def is_pair(q):
            return 0 <= q < NP

        def run(iteration):
            for t in range(NP + 1):
                iteration(t)

        @block.sync
        def _(sp):
            def load(g, par):
                if is_group(g):
                    reach(sp, centred, g - 1)
                    reach(sp, x_ordered, g - 1)
                    sp.dma_start(x_in[:, par], x_dram[g]).then_inc(x_loaded[par], 16)

            for par in range(2):
                load(par, par)
            for b in range(GB):
                sp.dma_start(wsel[C * b:C * b + C, :], W_sel).then_inc(c_loaded, 16)
                sp.dma_start(gate_rows[E * b:E * b + E, :], gate_w).then_inc(c_loaded, 16)
            for b in range(PB):
                sp.dma_start(gateb[E * b:E * b + E, :],
                             gate_b.rearrange("(e a) -> e a", a=1)).then_inc(c_loaded, 16)
            sp.dma_start(bsel[:], b_sel.rearrange("(a k) -> a k", a=1).broadcast_to([P, ROTS])
                         ).then_inc(c_loaded, 16)

            sp.dma_start(b2_rows[:], weight2[:, H, :]).then_inc(c_loaded, 16)
            for g in range(2, NG):
                load(g, g % 2)
            sp.dma_start(w1[:], weight1.rearrange("e c h -> c e h")).then_inc(w_loaded, 16)
            sp.dma_start(w2[:], weight2[:, 0:H, :].rearrange("e h o -> h e o")).then_inc(w_loaded, 16)

            for q in range(NP):
                for s in range(SH):
                    sp.wait_ge(added, (q * SH + s + 1) * (J // 2))
                    b = slice(q * PB, q * PB + PB)
                    sp.dma_start(out_dram[:, b, s], x1[:, b, s].rearrange("p b j c -> p b (j c)")
                                 ).then_inc(stored, 16)
            sp.wait_ge(stored, 16 * NP * SH)

        N_CONST = 16 * (2 * GB + PB + 2)

        @block.gpsimd
        def _(pool):
            link = Links(pool, mask_link, 8)
            link.begin(0)
            link.then(pool.memset(ident[:], 0.0))
            link.then(pool.memset(same_image[:], 1.0))
            link.then(pool.memset(own_slot[:], 1.0))
            link.then(pool.memset(slots_c[C:C + 1], 1.0))
            link.then(pool.affine_select(out=ident[:], in_=ident[:], compare_op=ALU.not_equal, fill=1.0,
                                         base=0, pattern=[[-1, P]], channel_multiplier=1))
            v = same_image[:].rearrange("p (b c) -> p b c", c=C)
            link.then(pool.affine_select(out=v, in_=v, compare_op=ALU.is_ge, fill=0.0, base=0,
                                         pattern=[[-C, GB], [0, C]], channel_multiplier=1))
            link.then(pool.affine_select(out=v, in_=v, compare_op=ALU.is_ge, fill=0.0, base=C - 1,
                                         pattern=[[C, GB], [0, C]], channel_multiplier=-1))
            link.then(pool.affine_select(out=own_slot[:], in_=own_slot[:], compare_op=ALU.is_ge, fill=0.0,
                                         base=0, pattern=[[-E, PB], [0, O]], channel_multiplier=1))
            link.end()
            pool.affine_select(out=own_slot[:], in_=own_slot[:], compare_op=ALU.is_ge, fill=0.0,
                               base=E - 1, pattern=[[E, PB], [0, O]], channel_multiplier=-1
                               ).then_inc(masks, 1)

            def centre_tokens(g, par):
                if is_group(g):
                    pool.wait_ge(mean1_ready, g + 1)
                    reach(pool, y_turned, SH * (g - 1))
                    m = mean1[:, par].rearrange("p (b k) -> p b k", b=GB)
                    pool.tensor_tensor(y_tok[:, par].rearrange("p k b c -> p b k c"),
                                       x_in[:, par].rearrange("p b s (j c) -> p b (s j) c", c=C),
                                       m.unsqueeze(3).broadcast_to([P, GB, SH * J, C]), ALU.subtract
                                       ).then_inc(centred, 1)

            def take_top(q):
                if is_pair(q):
                    reach(pool, take_turned, SH * q)
                    reach(pool, take_kept, q)
                    pool.wait_ge(rest_ready, 2 * q + 2)
                    pool.tensor_tensor(picked[:], prob[:], rest[:], ALU.subtract
                                       ).then_inc(picked_ready, 1)
                    pool.wait_ge(picked_ready, q + 1)
                    pool.tensor_scalar(take[:], picked[:], rden[:, 0:1], 1.0, ALU.mult, ALU.mult
                                       ).then_inc(take_ready, 1)

            def iteration(t):
                centre_tokens(2 * t, 0)
                centre_tokens(2 * t + 1, 1)
                take_top(t - 1)

            run(iteration)

        @block.scalar
        def _(act):
            def square_input(g, par):
                if is_group(g):
                    act.wait_ge(centred, g + 1)
                    reach(act, square1_used, g)
                    act.activation(square1[:], y_tok[:, par].rearrange("p k b c -> p (k b c)"), ACT.Square
                                   ).then_inc(square1_ready, 1)

            def order_input(g, par):
                if is_group(g):
                    act.wait_ge(mean1_ready, g + 1)
                    reach(act, x_turned, g - 1)
                    act.activation(x_cols[:, par].rearrange("p k b c -> p b k c"),
                                   x_in[:, par].rearrange("p b s (j c) -> p b (s j) c", c=C), ACT.Copy
                                   ).then_inc(x_ordered, 1)

            def rsqrt_input(g):
                if is_group(g):
                    act.wait_ge(var1_ready, g + 1)
                    act.activation(ln1[:], var1[:], ACT.Ln).then_inc(ln1_link, 1)
                    act.wait_ge(ln1_link, g + 1)
                    act.activation(r1[:], ln1[:], ACT.Exp, scale=-0.5).then_inc(r1_ready, 1)

            def keep_y(g, par):
                if is_group(g):
                    for s in range(SH):
                        act.wait_ge(y_turned, SH * g + s + 1)
                        if s == 0:
                            reach(act, conv_done, SH * (g - 1))
                            reach(act, x1_ready, SH * (g - 1))
                        act.activation(
                            y_chan[:, par, s * BANK:(s + 1) * BANK].rearrange("p (k j) -> p j k", j=J),
                            psum[:, TURN + s].rearrange("p (j k) -> p j k", j=J), ACT.Copy,
                            accum_out=chan_sum[:, par, s:s + 1]).then_inc(y_chan_ready, 1)

            def exp_rot(g):
                if is_group(g):
                    act.wait_ge(rot_nmax_ready, g + 1)
                    act.activation(rot_exp[:], rot_logit[:], ACT.Exp, bias=rot_nmax[:, 0:1],
                                   accum_out=rot_den[:, 0:1]).then_inc(rot_exp_ready, 1)

            def keep_x1(g):
                if is_group(g):
                    for s in range(SH):
                        act.wait_ge(x1_turned, SH * g + s + 1)
                        if s == 0:
                            reach(act, square2_used, g)
                        turned = psum[:, TURN + s].rearrange("p (j b c) -> p b j c", j=J, c=C)
                        act.activation(square2[:, :, s], turned, ACT.Square).then_inc(square2_ready, 1)
                        act.activation(x1[:, bass.ds(g * GB, GB), s], turned, ACT.Copy
                                       ).then_inc(x1_kept, 1)

            def rsqrt_tokens(g):
                if is_group(g):
                    act.wait_ge(var2_ready, g + 1)
                    act.activation(ln2[:], var2[:], ACT.Ln).then_inc(ln2_link, 1)
                    act.wait_ge(ln2_link, g + 1)
                    act.activation(r2[:], ln2[:], ACT.Exp, scale=-0.5).then_inc(r2_ready, 1)

            def exp_slots(q):
                if is_pair(q):
                    act.wait_ge(neg_max_ready, q + 1)
                    reach(act, picked_ready, q)
                    reach(act, take_ready, q)
                    act.activation(prob[:].rearrange("p (s k j) -> p s j k", s=SH, j=J),
                                   psum[:, ROWS:ROWS + SH].rearrange("p s (j k) -> p s j k", j=J),
                                   ACT.Exp, bias=neg_max[:, 0:1], accum_out=den[:, 0:1]
                                   ).then_inc(prob_ready, 1)
                    act.activation(top_e[:], top[:], ACT.Exp, bias=neg_max[:, 0:1]
                                   ).then_inc(prob_ready, 1)

            def keep_take(q):
                if is_pair(q):
                    act.wait_ge(take_ready, q + 1)
                    act.activation(take_all[:, bass.ds(q, 1)].rearrange("p a s -> p (a s)"), take[:], ACT.Copy
                                   ).then_inc(take_kept, 1)

            act.preload_act_table_set("natural_log_exp_and_others")

            def iteration(t):
                order_input(2 * t, 0)
                square_input(2 * t, 0)
                keep_y(2 * t - 1, 1)
                keep_x1(2 * t - 2)
                rsqrt_input(2 * t)
                exp_rot(2 * t - 1)
                rsqrt_tokens(2 * t - 2)
                order_input(2 * t + 1, 1)
                square_input(2 * t + 1, 1)
                keep_y(2 * t, 0)
                keep_x1(2 * t - 1)
                exp_rot(2 * t)
                rsqrt_tokens(2 * t - 1)
                rsqrt_input(2 * t + 1)
                exp_slots(t - 1)
                keep_take(t - 1)

            run(iteration)

            act.preload_act_table(ACT.Gelu)
            for i in range(E // 4):
                act.wait_ge(hidden_done, i + 1)
                act.activation(hidden[:, 4 * i:4 * i + 4].rearrange("p e b -> p (e b)"),
                               psum[:, HIDDEN_BANKS[i], 0:4 * B], ACT.Gelu).then_inc(hidden_ready, 1)

        @block.vector
        def _(dve):
            dve.wait_ge(masks, 1)
            dve.tensor_scalar(gate_mean[:, GB * E:LC],
                              same_image[:].rearrange("p (b c) -> p c b", c=C)[:, 0], 1.0 / C, None,
                              ALU.mult).then_inc(gate_set, 1)

            dve.wait_ge(c_loaded, N_CONST)
            gate_l = Links(dve, gate_link, 3)
            gate_l.begin(0)
            gate_l.then(dve.tensor_reduce(gate_sum[:], gate_rows[:], AX.X, ALU.add))
            gate_l.then(dve.tensor_scalar(gate_avg[:], gate_sum[:], 1.0 / C, None, ALU.mult))
            gate_l.then(dve.tensor_scalar(gate_cent[:], gate_rows[:], gate_avg[:, 0:1], None, ALU.subtract))
            gate_l.end()
            dve.tensor_tensor(gate_diag[:], own_slot[0:GB * E, 0:GB],
                              gate_cent[:].unsqueeze(1).broadcast_to([GB * E, GB, C]), ALU.mult
                              ).then_inc(gate_diag_ready, 1)

            def gate_columns():
                dve.wait_ge(gate_turned, 1)
                dve.tensor_copy(gate_mean[:, 0:GB * E], psum[:, LOGI, 0:GB * E]).then_inc(gate_ready, 1)
                dve.tensor_copy(b2[:], psum[0:O, LOGI + 1, 0:E]).then_inc(gate_ready, 1)

            mean1_l = Links(dve, mean1_link, 1)
            norm1_l = Links(dve, norm1_link, 3)
            pool_l = Links(dve, pool_link, 1)
            rot_l = Links(dve, rot_link, 1)
            rot_w_l = Links(dve, rot_w_link, 2)
            stat2_l = Links(dve, stat2_link, 4)
            norm2_l = Links(dve, norm2_link, 3)
            max_l = Links(dve, max_link, 2)
            gather_l = Links(dve, gather_link, 2)

            def newton(link, n, v, r, tmp, out_, last=None):
                link.begin(n)
                link.then(dve.tensor_tensor(tmp[:, 0], r, r, ALU.mult))
                link.then(dve.scalar_tensor_tensor(tmp[:, 1], tmp[:, 0], -0.5, v, ALU.mult, ALU.mult))
                link.then(dve.scalar_tensor_tensor(out_, tmp[:, 1], 1.5, r, ALU.add, ALU.mult))
                link.end()

            def mean_input(g, par):
                if is_group(g):
                    dve.wait_ge(x_loaded[par], 16 * (g // 2 + 1))
                    mean1_l.begin(g)
                    mean1_l.then(dve.tensor_reduce(sum1[:], token_groups(x_in[:, par]), AX.X, ALU.add))
                    mean1_l.end()
                    dve.tensor_scalar(mean1[:, par], sum1[:], 1.0 / C, None, ALU.mult
                                      ).then_inc(mean1_ready, 1)

            def var_input(g):
                if is_group(g):
                    dve.wait_ge(square1_ready, g + 1)
                    dve.tensor_reduce(ssum1[:], square1[:].rearrange("p (k c) -> p k c", c=C), AX.X, ALU.add
                                      ).then_inc(square1_used, 1)
                    dve.wait_ge(square1_used, g + 1)
                    dve.tensor_scalar(var1[:], ssum1[:], 1.0 / C, EPS_IN, ALU.mult, ALU.add
                                      ).then_inc(var1_ready, 1)

            def norm_input(g, par):
                if is_group(g):
                    dve.wait_ge(r1_ready, g + 1)
                    newton(norm1_l, g, var1[:], r1[:], n1, rstd1[:])
                    y = y_tok[:, par].rearrange("p k b c -> p (k b) c")
                    dve.tensor_tensor(y, y, spread_over(rstd1[:], C), ALU.mult).then_inc(y_ready, 1)

            def pool_image(g, par):
                if is_group(g):
                    dve.wait_ge(y_chan_ready, SH * g + SH)
                    pool_l.begin(g)
                    pool_l.then(dve.tensor_tensor(pooled[:], chan_sum[:, par, 0:1], chan_sum[:, par, 1:2],
                                                  ALU.add))
                    pool_l.end()
                    dve.tensor_scalar(wsel_rhs[:], wsel[:], pooled[:, 0:1], 1.0 / S, ALU.mult, ALU.mult
                                      ).then_inc(wsel_rhs_ready, 1)

            def rot_max(g):
                if is_group(g):
                    dve.wait_ge(rot_logits, g + 1)
                    rot_l.begin(g)
                    rot_l.then(dve.tensor_tensor(rot_logit[:], psum[:, ROWS, 0:ROTS], bsel[:], ALU.add))
                    rot_l.end()
                    dve.tensor_reduce(rot_nmax[:], rot_logit[:], AX.X, ALU.max, negate=True
                                      ).then_inc(rot_nmax_ready, 1)

            def rot_weights(g, par):
                if is_group(g):
                    dve.wait_ge(rot_exp_ready, g + 1)
                    rot_w_l.begin(g)
                    rot_w_l.then(dve.reciprocal(rot_rden[:], rot_den[:]))
                    rot_w_l.then(dve.tensor_scalar(rot_w[:, par], rot_exp[:], rot_rden[:, 0:1], None,
                                                   ALU.mult))
                    rot_w_l.end()
                    for i in range(2):
                        dve.tensor_scalar(diag[:, i], ident[:], rot_w[:, par, 2 * i + 1:2 * i + 2], None,
                                          ALU.mult).then_inc(diag_ready, 1)

            def add_turns(g, par):
                if is_group(g):
                    y = y_chan[:, par]
                    for s in range(SH):
                        dve.wait_ge(conv_done, SH * g + s + 1)
                        if s == 0:
                            reach(dve, logits_done, SH * (g - 1))
                        o = x1_chan[:, par, s]
                        dve.scalar_tensor_tensor(
                            o, y[:, s * BANK:(s + 1) * BANK].rearrange("p (k j) -> p j k", j=J),
                            rot_w[:, par, 0:1], psum[:, CONV + s].rearrange("p (j k) -> p j k", j=J),
                            ALU.mult, ALU.add).then_inc(conv_used, 1)
                    for s in range(SH):
                        dve.wait_ge(conv_used, SH * g + s + 1)
                        o = x1_chan[:, par, s]
                        back = y[:, ::-1][:, s * BANK:(s + 1) * BANK]
                        dve.scalar_tensor_tensor(
                            o, back.rearrange("p (k j) -> p j k", j=J), rot_w[:, par, 2:3], o,
                            ALU.mult, ALU.add).then_inc(x1_ready, 1)

            def var_tokens(g):
                if is_group(g):
                    dve.wait_ge(square2_ready, SH * g + SH)
                    stat2_l.begin(g)
                    dve.tensor_reduce(ssum2[:], square2[:].rearrange("p b s j c -> p (b s j) c"), AX.X,
                                      ALU.add).then_inc(square2_used, 1)
                    dve.wait_ge(square2_used, g + 1)
                    for s in range(SH):
                        dve.wait_ge(logits_done, SH * g + s + 1)
                        m = psum[:, LOGI + s, 0:J * LC].rearrange("p (j k) -> p j k", k=LC)[:, :, GB * E:LC]
                        stat2_l.then(dve.tensor_copy(mean2[:, :, s].rearrange("p b j -> p j b"), m))
                    m = mean2[:].rearrange("p b s j -> p (b s j)")
                    stat2_l.then(dve.tensor_tensor(msq2[:], m, m, ALU.mult))
                    stat2_l.then(dve.scalar_tensor_tensor(vraw2[:], ssum2[:], 1.0 / C, msq2[:], ALU.mult,
                                                          ALU.subtract))
                    stat2_l.end()
                    dve.tensor_scalar(var2[:], vraw2[:], 0.0, EPS_TOK, ALU.max, ALU.add
                                      ).then_inc(var2_ready, 1)

            def norm_logits(g, par, q):
                if is_group(g):
                    dve.wait_ge(r2_ready, g + 1)
                    r = rstd2[:, par]
                    newton(norm2_l, g, var2[:], r2[:], n2, r.rearrange("p b s j -> p (b s j)"))
                    reach(dve, rows_done, q)
                    for s in range(SH):
                        dve.tensor_tensor(
                            logit_tok[:, s * J:s * J + J, par],
                            psum[:, LOGI + s, 0:J * LC].rearrange("p (j k) -> p j k", k=LC)[:, :, 0:GB * E]
                            .rearrange("p j (b e) -> p j b e", e=E),
                            r[:, :, s].rearrange("p b j -> p j b").unsqueeze(3)
                            .broadcast_to([P, J, GB, E]), ALU.mult).then_inc(logit_ready, 1)

            def row_max(q):
                if is_pair(q):
                    dve.wait_ge(rows_done, q + 1)
                    max_l.begin(q)
                    max_l.then(dve.max(top[:], psum[:, ROWS:ROWS + SH].rearrange("p s k -> p (s k)")))
                    max_l.then(dve.tensor_tensor(gb_max[:], top[:, 0:1], gateb[:], ALU.add))
                    max_l.end()
                    dve.tensor_tensor(neg_max[:], gateb[:], gb_max[:], ALU.subtract
                                      ).then_inc(neg_max_ready, 1)

            def remove_top(q):
                if is_pair(q):
                    dve.wait_ge(prob_ready, 2 * q + 2)
                    reach(dve, take_ready, q)
                    dve.reciprocal(rden[:], den[:]).then_inc(rest_ready, 1)
                    dve.match_replace(rest[:], top_e[:], prob[:], 0.0).then_inc(rest_ready, 1)

            def turn_take(q):
                if is_pair(q):
                    reach(dve, gathered, q)
                    for s in range(SH):
                        dve.wait_ge(take_turned, SH * q + s + 1)
                        dve.tensor_tensor(
                            take_tok[:, s * J:s * J + J],
                            psum[:, ROWS + s].rearrange("p (j b e) -> p j b e", j=J, e=E),
                            rstd2[:].rearrange("p g b s j -> p s j (g b)")[:, s].unsqueeze(3)
                            .broadcast_to([P, J, PB, E]), ALU.mult).then_inc(take_tok_ready, 1)

            def keep_slots(q):
                if is_pair(q):
                    dve.wait_ge(gathered, q + 1)
                    got = psum[0:E, LOGI, 0:PB * C].rearrange("p (b c) -> p b c", c=C)
                    gather_l.begin(q)
                    gather_l.then(dve.tensor_reduce(slot_sum[:], got, AX.X, ALU.add))
                    gather_l.then(dve.tensor_scalar(slot_mean[:], slot_sum[:], 1.0 / C, None, ALU.mult))
                    gather_l.end()
                    dve.tensor_tensor(slots[:, bass.ds(q * PB, PB)], got,
                                      slot_mean[:].unsqueeze(2).broadcast_to([E, PB, C]), ALU.subtract
                                      ).then_inc(slots_ready, 1)

            def iteration(t):
                mean_input(2 * t, 0)
                pool_image(2 * t - 1, 1)
                var_input(2 * t)
                var_tokens(2 * t - 2)
                rot_max(2 * t - 1)
                norm_input(2 * t, 0)
                rot_weights(2 * t - 1, 1)
                norm_logits(2 * t - 2, 0, t - 1)
                mean_input(2 * t + 1, 1)
                add_turns(2 * t - 1, 1)
                pool_image(2 * t, 0)
                if t == 0:
                    gate_columns()
                rot_max(2 * t)
                var_tokens(2 * t - 1)
                var_input(2 * t + 1)
                rot_weights(2 * t, 0)
                norm_logits(2 * t - 1, 1, t - 1)
                norm_input(2 * t + 1, 1)
                row_max(t - 1)
                add_turns(2 * t, 0)
                remove_top(t - 1)
                turn_take(t - 1)
                keep_slots(t - 1)

            run(iteration)

            dve.wait_ge(slots_turned, 1)
            dve.tensor_copy(slots_c[0:C].rearrange("p b e -> p (b e)"), psum[0:C, TURN]
                            ).then_inc(slots_c_ready, 1)
            dve.wait_ge(slot_out_done, 1)
            dve.tensor_tensor(slot_out[:], psum[0:O, OUT_BANK].rearrange("p (e b) -> p b e", b=B),
                              b2[:].unsqueeze(1).broadcast_to([O, B, E]), ALU.add
                              ).then_inc(slot_out_ready, 1)
            dve.wait_ge(slot_out_turned, 1)
            for q in range(NP):
                dve.tensor_tensor(spread[:, q],
                                  psum[:, TURN + 1, q * O:q * O + O].unsqueeze(1).broadcast_to([P, PB, O]),
                                  own_slot[:], ALU.mult).then_inc(spread_ready, 1)
            n = 0
            for q in range(NP):
                for s in range(SH):
                    for j in range(0, J, 2):
                        dve.wait_ge(scattered, n + 1)
                        v = x1[:, q * PB:q * PB + PB, s, j:j + 2].rearrange("p b j c -> p j b c")
                        dve.tensor_tensor(v, psum[:, n % 8].rearrange("p (j b c) -> p j b c", j=2, c=O), v,
                                          ALU.add).then_inc(added, 1)
                        n += 1

        @block.tensor
        def _(pe):
            pe.wait_ge(masks, 1)
            pe.wait_ge(gate_diag_ready, 1)
            pe.transpose(psum[:, LOGI, 0:GB * E], gate_diag[:].rearrange("p b c -> p (b c)"),
                         ident[0:GB * E, 0:GB * E])
            pe.transpose(psum[0:O, LOGI + 1, 0:E], b2_rows[:], ident[0:E, 0:E]).then_inc(gate_turned, 1)

            def turn(out_, in_, start):
                return pe.matmul(out_, in_, ident[:], start=start, stop=True, is_transpose=True)

            def turn_input(g, par):
                if is_group(g):
                    pe.wait_ge(y_ready, g + 1)
                    def columns(t, s, j):
                        return t[:, par, s * J + j].rearrange("p b c -> p (b c)")

                    for s in range(SH):
                        reach(pe, x1_kept, SH * (g - 2) + s + 1)
                        for j in range(J):
                            mm = pe.transpose(psum[:, TURN + s, j * P:j * P + P], columns(y_tok, s, j), ident[:])
                        mm.then_inc(y_turned, 1)
                    pe.wait_ge(x_ordered, g + 1)
                    for s in range(SH):
                        reach(pe, conv_used, SH * (g - 1) + s + 1)
                        for j in range(J):
                            mm = pe.matmul(psum[:, CONV + s, j * P:j * P + P], columns(x_cols, s, j), ident[:],
                                           start=(j == 0), stop=False, is_transpose=True,
                                           skip_group_check=True)
                    mm.then_inc(x_turned, 1)

            def rot_select(g):
                if is_group(g):
                    pe.wait_ge(wsel_rhs_ready, g + 1)
                    pe.matmul(psum[:, ROWS, 0:ROTS], same_image[:], wsel_rhs[:], start=True, stop=True
                              ).then_inc(rot_logits, 1)

            def add_odd_turns(g, par):
                if is_group(g):
                    pe.wait_ge(diag_ready, 2 * g + 2)
                    img = y_chan[:, par].rearrange("p (h w) -> p h w", w=WW)
                    t1 = img[:, :, ::-1].rearrange("p (v j) h -> p j h v", j=J)
                    t3 = img[:, ::-1, :].rearrange("p (v j) h -> p j h v", j=J)
                    hs = HH // SH
                    for s in range(SH):
                        for i, t in enumerate((t1, t3)):
                            mm = pe.matmul(psum[:, CONV + s], diag[:, i], t[:, :, s * hs:s * hs + hs],
                                           start=False, stop=(i == 1), skip_group_check=True)
                        mm.then_inc(conv_done, 1)

            def turn_x1(g, par):
                if is_group(g):
                    for s in range(SH):
                        pe.wait_ge(x1_ready, SH * g + s + 1)
                        pe.wait_ge(y_chan_ready, min(SH * (g + 1) + s + 1, SH * NG))
                        for j in range(J):
                            mm = pe.transpose(psum[:, TURN + s, j * P:j * P + P], x1_chan[:, par, s, j],
                                              ident[:])
                        mm.then_inc(x1_turned, 1)

            def gate_logits(g, par, q):
                if is_group(g):
                    if g == 0:
                        pe.wait_ge(gate_ready, 2)
                        pe.wait_ge(gate_set, 1)
                    for s in range(SH):
                        reach(pe, logit_ready, SH * (g - 1) + s + 1)
                        if par == 0:
                            reach(pe, slots_ready, q)
                        for j in range(J):
                            mm = pe.matmul(psum[:, LOGI + s, j * LC:j * LC + LC], x1_chan[:, par, s, j],
                                           gate_mean[:], start=True, stop=True)
                        mm.then_inc(logits_done, 1)

            def turn_logits(q):
                if is_pair(q):
                    pe.wait_ge(logit_ready, 2 * SH * q + 2 * SH)
                    for k in range(SH * J):
                        mm = pe.transpose(psum[:, ROWS + k // J, (k % J) * P:(k % J + 1) * P],
                                          logit_tok[:, k].rearrange("p g b e -> p (g b e)"), ident[:])
                    mm.then_inc(rows_done, 1)

            def turn_take(q):
                if is_pair(q):
                    pe.wait_ge(take_ready, q + 1)
                    rows = take[:].rearrange("p (s k j) -> p s j k", s=SH, j=J)
                    for s in range(SH):
                        for j in range(J):
                            mm = pe.transpose(psum[:, ROWS + s, j * P:j * P + P], rows[:, s, j], ident[:])
                        mm.then_inc(take_turned, 1)

            def gather(q):
                if is_pair(q):
                    pe.wait_ge(take_tok_ready, SH * q + SH)
                    pe.wait_ge(x1_kept, 2 * SH * q + 2 * SH)
                    for b in range(PB):
                        for k in range(SH * J):
                            mm = pe.matmul(psum[0:E, LOGI, b * C:b * C + C], take_tok[:, k, b],
                                           x1[:, bass.ds(q * PB + b, 1), k // J, k % J]
                                           .rearrange("p a c -> p (a c)"),
                                           start=(k == 0), stop=(k == SH * J - 1))
                    mm.then_inc(gathered, 1)

            def iteration(t):
                turn_input(2 * t - 1, 1)
                turn_x1(2 * t - 2, 0)
                rot_select(2 * t - 1)
                gate_logits(2 * t - 2, 0, t - 1)
                add_odd_turns(2 * t - 1, 1)
                turn_input(2 * t, 0)
                turn_x1(2 * t - 1, 1)
                gate_logits(2 * t - 1, 1, t - 1)
                rot_select(2 * t)
                turn_logits(t - 1)
                add_odd_turns(2 * t, 0)
                turn_take(t - 1)
                gather(t - 1)

            run(iteration)

            pe.wait_ge(slots_ready, NP)
            for b in range(B):
                mm = pe.transpose(psum[0:C, TURN, b * E:b * E + E], slots[:, b], ident[0:E, 0:E])
            mm.then_inc(slots_turned, 1)
            pe.wait_ge(w_loaded, 32)
            pe.wait_ge(slots_c_ready, 1)
            for e in range(E):
                mm = pe.matmul(psum[:, HIDDEN_BANKS[e // 4], (e % 4) * B:(e % 4 + 1) * B], w1[:, e],
                               slots_c[:, :, e], start=True, stop=True)
                if e % 4 == 3:
                    mm.then_inc(hidden_done, 1)
            for e in range(E):
                if e % 4 == 0:
                    pe.wait_ge(hidden_ready, e // 4 + 1)
                mm = pe.matmul(psum[0:O, OUT_BANK, e * B:e * B + B], w2[:, e], hidden[:, e],
                               start=True, stop=True)
            mm.then_inc(slot_out_done, 1)
            pe.wait_ge(slot_out_ready, 1)
            for q in range(NP):
                mm = pe.transpose(psum[:, TURN + 1, q * O:q * O + O],
                                  slot_out[:, q * PB:q * PB + PB].rearrange("p b e -> p (b e)"),
                                  ident[0:O, 0:O])
            mm.then_inc(slot_out_turned, 1)
            n = 0
            for q in range(NP):
                pe.wait_ge(spread_ready, NP if q == 0 else q + 1)
                pe.wait_ge(take_kept, NP)
                rows = take_all[:, q].rearrange("p (s k j) -> p s j k", s=SH, j=J)
                for s in range(SH):
                    for j in range(J):
                        if j % 2 == 0:
                            reach(pe, added, n - 7)
                        mm = pe.matmul(psum[:, n % 8, (j % 2) * PB * O:(j % 2 + 1) * PB * O], rows[:, s, j],
                                       spread[:, q].rearrange("p b o -> p (b o)"), start=True, stop=True)
                        if j % 2 == 1:
                            mm.then_inc(scattered, 1)
                            n += 1


_INS = ["x", "L0_conv_W_sel", "L0_conv_b_sel", "L0_ffn_gate_w", "L0_ffn_gate_b", "L0_ffn_weight1", "L0_ffn_weight2"]
_OUTS = [((32, 32, 32, 32), "float32")]


def kernel(**inputs):
    import numpy as _np
    import concourse.bacc as _bacc
    from concourse import mybir as _mybir
    from concourse.bass_utils import run_bass_kernel_spmd as _run

    nc = _bacc.Bacc("TRN2", target_bir_lowering=False, num_devices=1)
    arrays, args = {}, []
    for name in _INS:
        a = _np.ascontiguousarray(inputs[name])
        arrays[f"in_{name}_dram"] = a
        args.append(nc.dram_tensor(f"in_{name}_dram", a.shape, _mybir.dt.from_np(a.dtype), kind="ExternalInput").ap())
    for i, (shape, dtype) in enumerate(_OUTS):
        dt = _mybir.dt.from_np(_np.dtype(dtype))
        args.append(nc.dram_tensor(f"out_{i}_dram", shape, dt, kind="ExternalOutput").ap())
    rotate_and_route_kernel(nc, *args)
    r = _run(nc, [arrays], core_ids=[0])
    return r.results[0]["out_0_dram"]
```

```python
from contextlib import ExitStack

import concourse.bass as bass
from concourse import mybir

ALU = mybir.AluOpType
ACT = mybir.ActivationFunctionType
AX = mybir.AxisListType
F32 = mybir.dt.float32

P = 128
BANK = 512
TOPK = 8
ROTS = 4
EPS_IN = 1e-6
EPS_TOK = 1e-5


class Links:

    def __init__(self, eng, sem, per):
        self.eng, self.sem, self.per = eng, sem, per

    def begin(self, n):
        self.base, self.i = n * self.per, 0

    def then(self, ins):
        self.i += 1
        ins.then_inc(self.sem, 1)
        self.eng.wait_ge(self.sem, self.base + self.i)

    def end(self):
        assert self.i == self.per, (self.i, self.per)


def reach(eng, sem, value):
    if value > 0:
        eng.wait_ge(sem, value)


def rotate_and_route_kernel(
    nc: bass.Bass,
    x: bass.AP,
    W_sel: bass.AP,
    b_sel: bass.AP,
    gate_w: bass.AP,
    gate_b: bass.AP,
    weight1: bass.AP,
    weight2: bass.AP,
    out: bass.AP,
):
    B, HH, WW, C = x.shape
    E, _, H = weight1.shape
    O = weight2.shape[2]
    S = HH * WW
    GB = P // C
    NG = B // GB
    NP = NG // 2
    SH = S // BANK
    J = BANK // P
    K = SH * J
    GT = GB * K
    PB = 2 * GB
    LC = GB * E + GB
    WAVES = [(0, NP - 1), (NP - 1, NP)]
    assert (HH, WW, C, E, H, O) == (32, 32, 32, 16, 128, 32) and PB * E == P and NG % 2 == 0

    with ExitStack() as ctx:
        def sb(name, shape):
            return ctx.enter_context(nc.sbuf_tensor(name, shape, F32))

        def sem(name):
            return ctx.enter_context(nc.semaphore(name))

        psum = ctx.enter_context(nc.psum_tensor("psum", [P, 8, BANK], F32))
        TURN, CONV, LOGI, ROWS = 0, 2, 4, 6
        ROT_AT = J * LC

        ident = sb("ident", [P, P])
        same_image = sb("same_image", [P, P])
        own_slot = sb("own_slot", [P, PB, O])
        eps_in = sb("eps_in", [P, 1])
        gate_rows = sb("gate_rows", [GB * E, C])
        gate_sum = sb("gate_sum", [GB * E, 1])
        gate_avg = sb("gate_avg", [GB * E, 1])
        gate_cent = sb("gate_cent", [GB * E, C])
        gate_diag = sb("gate_diag", [GB * E, GB, C])
        gate_mean = sb("gate_mean", [P, LC])
        wsel = sb("wsel", [P, ROTS])
        bsel = sb("bsel", [P, ROTS])
        gateb = sb("gateb", [P, 1])
        w1 = sb("w1", [C + 1, E, H])
        w2 = sb("w2", [H, E, O])
        b2_rows = sb("b2_rows", [E, O])
        b2 = sb("b2", [O, E])
        centre = sb("centre", [C, C])

        x_in = sb("x_in", [P, 2, GB, SH, J * C])
        x_cols = sb("x_cols", [P, 2, K, GB, C])
        y_tok = sb("y_tok", [P, 2, K, GB, C])
        square1 = sb("square1", [P, K * GB * C])
        y_chan = sb("y_chan", [P, 2, S])
        turn0 = sb("turn0", [P, S])
        turn2 = sb("turn2", [P, S])
        even_turns = sb("even_turns", [P, S])
        x1_chan = sb("x1_chan", [P, 2, SH, J, P])
        square2 = sb("square2", [P, GB, SH, J, C])

        sum1 = sb("sum1", [P, NG, GT])
        mean1 = sb("mean1", [P, NG, GT])
        ssum1 = sb("ssum1", [P, NG, GT])
        var1 = sb("var1", [P, NG, GT])
        ln1 = sb("ln1", [P, NG, GT])
        r1 = sb("r1", [P, NG, GT])
        n1 = sb("n1", [P, 3, NG, GT])
        rstd1 = sb("rstd1", [P, NG, GT])
        chan_sum = sb("chan_sum", [P, NG])
        wsel_rhs = sb("wsel_rhs", [P, NG, ROTS])
        rot_logit = sb("rot_logit", [P, NG, ROTS])
        rot_nmax = sb("rot_nmax", [P, NG])
        rot_exp = sb("rot_exp", [P, NG, ROTS])
        rot_den = sb("rot_den", [P, NG])
        rot_rden = sb("rot_rden", [P, NG])
        rot_w = sb("rot_w", [P, NG, ROTS])
        diag = sb("diag", [P, 2, P])
        ssum2 = sb("ssum2", [P, NG, GT])
        msq2 = sb("msq2", [P, NG, GB, SH, J])
        avg2 = sb("avg2", [P, NG, GT])
        vraw2 = sb("vraw2", [P, NG, GT])
        var2 = sb("var2", [P, NG, GT])
        ln2 = sb("ln2", [P, NG, GT])
        r2 = sb("r2", [P, NG, GT])
        n2 = sb("n2", [P, 3, NG, GT])
        rstd2 = sb("rstd2", [P, NG, GB, SH, J])

        logit_tok = sb("logit_tok", [P, K, 2, GB, E])
        top = sb("top", [P, NP, TOPK])
        top_e = sb("top_e", [P, NP, TOPK])
        gb_max = sb("gb_max", [P, NP])
        neg_max = sb("neg_max", [P, NP])
        den = sb("den", [P, NP])
        rden = sb("rden", [P, NP])
        prob = sb("prob", [P, S])
        rest = sb("rest", [P, S])
        picked = sb("picked", [P, S])
        take_tok = sb("take_tok", [P, K, PB, E])

        x1 = sb("x1", [P, B, SH, J, C])
        take = sb("take", [P, NP, S])
        slots = sb("slots", [C, B, E])
        slots_c = sb("slots_c", [C + 1, B, E])
        hidden = sb("hidden", [H, E, B])
        slot_out = sb("slot_out", [O, B, E])
        spread = sb("spread", [P, NP, PB, O])

        x_loaded = [sem("x_loaded_even"), sem("x_loaded_odd")]
        c_loaded = sem("constants_loaded")
        w_loaded = sem("expert_weights_loaded")
        mask_link = sem("mask_link")
        masks = sem("masks_made")
        gate_set = sem("gate_set")
        gate_link = sem("gate_link")
        gate_diag_ready = sem("gate_diag_ready")
        gate_turned = sem("gate_turned")
        gate_ready = sem("gate_ready")
        sum1_ready = sem("sum1_ready")
        mean1_ready = sem("mean1_ready")
        x_ordered = sem("x_ordered")
        centred = sem("centred")
        square1_ready = sem("square1_ready")
        ssum1_ready = sem("ssum1_ready")
        ln1_link = sem("ln1_link")
        r1_ready = sem("r1_ready")
        var1_ready = sem("var1_ready")
        norm1_link = sem("norm1_link")
        rstd1_ready = sem("rstd1_ready")
        y_ready = sem("y_ready")
        y_turned = sem("y_turned")
        x_turned = sem("x_turned")
        y_chan_ready = sem("y_chan_ready")
        wsel_rhs_ready = sem("wsel_rhs_ready")
        rot_logits = sem("rot_logits")
        rot_logit_ready = sem("rot_logit_ready")
        rot_nmax_ready = sem("rot_nmax_ready")
        rot_exp_ready = sem("rot_exp_ready")
        rot_rden_link = sem("rot_rden_link")
        rot_w_ready = sem("rot_w_ready")
        diag_ready = sem("diag_ready")
        turns_ready = sem("turns_ready")
        even_turns_ready = sem("even_turns_ready")
        conv_done = sem("conv_done")
        x1_ready = sem("x1_ready")
        x1_turned = sem("x1_turned")
        square2_ready = sem("square2_ready")
        ssum2_ready = sem("ssum2_ready")
        msq2_ready = sem("msq2_ready")
        x1_kept = sem("x1_kept")
        logits_done = sem("logits_done")
        stat2_link = sem("stat2_link")
        var2_ready = sem("var2_ready")
        ln2_link = sem("ln2_link")
        r2_ready = sem("r2_ready")
        norm2_link = sem("norm2_link")
        rstd2_ready = sem("rstd2_ready")
        logit_ready = sem("logit_ready")
        rows_done = sem("rows_done")
        max_link = sem("max_link")
        neg_max_ready = sem("neg_max_ready")
        prob_ready = sem("prob_ready")
        rest_ready = sem("rest_ready")
        picked_ready = sem("picked_ready")
        take_ready = sem("take_ready")
        take_turned = sem("take_turned")
        take_tok_ready = sem("take_tok_ready")
        gathered = sem("gathered")
        slots_ready = sem("slots_ready")
        slots_centred = sem("slots_centred")
        slots_c_ready = sem("slots_c_ready")
        hidden_done = sem("hidden_done")
        hidden_ready = sem("hidden_ready")
        slot_out_done = sem("slot_out_done")
        slot_out_ready = sem("slot_out_ready")
        slot_out_turned = sem("slot_out_turned")
        spread_ready = sem("spread_ready")
        scattered = sem("scattered")
        added = sem("added")
        stored = sem("stored")

        x_dram = x.rearrange("(g b) h w c -> g b (h w) c", b=GB).rearrange(
            "g b (s p j) c -> g p b s (j c)", p=P, j=J)
        out_dram = out.rearrange("b h w c -> b (h w) c").rearrange(
            "b (s p j) c -> p b s (j c)", p=P, j=J)

        block = ctx.enter_context(nc.Block())

        STEPS = NG + 2
        LAST = NP - 1
        HID = (CONV, ROWS)
        OUTS, SMALL = TURN + 1, TURN

        def groups(*stages):
            for stage, n in stages:
                if 0 <= n < (NP if stage.__name__.startswith("pair_") else NG):
                    stage(n)

        def pair_at(k, lag):
            return (k - lag - 1) // 2 if (k - lag - 1) % 2 == 0 else -1

        PAIR_SUMS = K // 2
        SUM_BANKS = 4

        def final_sum(n):
            return n // PAIR_SUMS, n // (J // 2) % SH, 2 * (n % (J // 2)), CONV + n % SUM_BANKS

        @block.sync
        def _(sp):
            def load(g):
                reach(sp, centred, g - 1)
                reach(sp, x_ordered, g - 1)
                sp.dma_start(x_in[:, g % 2], x_dram[g]).then_inc(x_loaded[g % 2], 16)

            load(0)
            load(1)
            for b in range(GB):
                sp.dma_start(gate_rows[E * b:E * b + E, :], gate_w).then_inc(c_loaded, 16)
            sp.dma_start(b2_rows[:], weight2[:, H, :]).then_inc(c_loaded, 16)
            for b in range(GB):
                sp.dma_start(wsel[C * b:C * b + C, :], W_sel).then_inc(c_loaded, 16)
            for b in range(PB):
                sp.dma_start(gateb[E * b:E * b + E, :],
                             gate_b.rearrange("(e a) -> e a", a=1)).then_inc(c_loaded, 16)
            sp.dma_start(bsel[:], b_sel.rearrange("(a k) -> a k", a=1).broadcast_to([P, ROTS])
                         ).then_inc(c_loaded, 16)
            for g in range(2, NG):
                load(g)
                if g == 3:
                    sp.dma_start(w1[:], weight1.rearrange("e c h -> c e h")).then_inc(w_loaded, 16)
                    sp.dma_start(w2[:], weight2[:, 0:H, :].rearrange("e h o -> h e o")
                                 ).then_inc(w_loaded, 16)

            for q in range(NP):
                for s in range(SH):
                    sp.wait_ge(added, (q * SH + s + 1) * (J // 2))
                    b = slice(q * PB, q * PB + PB)
                    sp.dma_start(out_dram[:, b, s], x1[:, b, s].rearrange("p b j c -> p b (j c)")
                                 ).then_inc(stored, 16)
            sp.wait_ge(stored, 16 * NP * SH)

        N_CONST = 16 * (2 * GB + PB + 2)

        @block.gpsimd
        def _(pool):
            link = Links(pool, mask_link, 9)
            link.begin(0)
            link.then(pool.memset(ident[:], 0.0))
            link.then(pool.memset(same_image[:], 1.0))
            link.then(pool.memset(own_slot[:], 1.0))
            link.then(pool.memset(slots_c[C:C + 1], 1.0))
            link.then(pool.memset(eps_in[:], EPS_IN))
            link.then(pool.affine_select(out=ident[:], in_=ident[:], compare_op=ALU.not_equal, fill=1.0,
                                         base=0, pattern=[[-1, P]], channel_multiplier=1))
            v = same_image[:].rearrange("p (b c) -> p b c", c=C)
            link.then(pool.affine_select(out=v, in_=v, compare_op=ALU.is_ge, fill=0.0, base=0,
                                         pattern=[[-C, GB], [0, C]], channel_multiplier=1))
            link.then(pool.affine_select(out=v, in_=v, compare_op=ALU.is_ge, fill=0.0, base=C - 1,
                                         pattern=[[C, GB], [0, C]], channel_multiplier=-1))
            link.then(pool.affine_select(out=own_slot[:], in_=own_slot[:], compare_op=ALU.is_ge, fill=0.0,
                                         base=0, pattern=[[-E, PB], [0, O]], channel_multiplier=1))
            link.end()
            pool.affine_select(out=own_slot[:], in_=own_slot[:], compare_op=ALU.is_ge, fill=0.0,
                               base=E - 1, pattern=[[E, PB], [0, O]], channel_multiplier=-1
                               ).then_inc(masks, 1)
            pool.tensor_scalar(centre[:], ident[0:C, 0:C], 1.0, -1.0 / C, ALU.mult, ALU.add
                               ).then_inc(masks, 1)

            norm1_l = Links(pool, norm1_link, 3)
            norm2_l = Links(pool, norm2_link, 3)
            stat2_l = Links(pool, stat2_link, 2)

            def centre_tokens(g):
                pool.wait_ge(sum1_ready, g + 1)
                pool.tensor_scalar(mean1[:, g], sum1[:, g], 1.0 / C, 0.0, ALU.mult, ALU.add
                                   ).then_inc(mean1_ready, 1)
                pool.wait_ge(mean1_ready, g + 1)
                reach(pool, y_turned, SH * (g - 1))
                m = mean1[:, g].rearrange("p (b k) -> p b k", b=GB)
                pool.tensor_tensor(y_tok[:, g % 2].rearrange("p k b c -> p b k c"),
                                   x_in[:, g % 2].rearrange("p b s (j c) -> p b (s j) c", c=C),
                                   m.unsqueeze(3).broadcast_to([P, GB, K, C]), ALU.subtract
                                   ).then_inc(centred, 1)

            def order_input(g):
                pool.wait_ge(sum1_ready, g + 1)
                reach(pool, x_turned, g - 1)
                pool.tensor_scalar(x_cols[:, g % 2].rearrange("p k b c -> p b k c"),
                                   x_in[:, g % 2].rearrange("p b s (j c) -> p b (s j) c", c=C),
                                   1.0, 0.0, ALU.mult, ALU.add).then_inc(x_ordered, 1)

            def newton(link, n, v, r, tmp, out_, ready):
                link.begin(n)
                link.then(pool.tensor_tensor(tmp[:, 0, n], r, r, ALU.mult))
                link.then(pool.tensor_tensor(tmp[:, 1, n], tmp[:, 0, n], v, ALU.mult))
                link.then(pool.tensor_scalar(tmp[:, 2, n], tmp[:, 1, n], -0.5, 1.5, ALU.mult, ALU.add))
                link.end()
                pool.tensor_tensor(out_, tmp[:, 2, n], r, ALU.mult).then_inc(ready, 1)

            def rstd_input(g):
                pool.wait_ge(ssum1_ready, g + 1)
                pool.tensor_scalar(var1[:, g], ssum1[:, g], 1.0 / C, EPS_IN, ALU.mult, ALU.add
                                   ).then_inc(var1_ready, 1)
                pool.wait_ge(r1_ready, g + 1)
                pool.wait_ge(var1_ready, g + 1)
                newton(norm1_l, g, var1[:, g], r1[:, g], n1, rstd1[:, g], rstd1_ready)

            def add_even_turns(g):
                pool.wait_ge(turns_ready, 2 * g + 2)
                reach(pool, x1_ready, g)
                pool.tensor_tensor(even_turns[:], turn0[:], turn2[:, ::-1], ALU.add
                                   ).then_inc(even_turns_ready, 1)

            def var_tokens(g):
                pool.wait_ge(ssum2_ready, g + 1)
                stat2_l.begin(g)
                stat2_l.then(pool.tensor_scalar(avg2[:, g], ssum2[:, g], 1.0 / C, 0.0, ALU.mult, ALU.add))
                pool.wait_ge(msq2_ready, SH * g + SH)
                stat2_l.then(pool.tensor_tensor(vraw2[:, g], avg2[:, g],
                                                msq2[:, g].rearrange("p b s j -> p (b s j)"), ALU.subtract))
                stat2_l.end()
                pool.tensor_scalar(var2[:, g], vraw2[:, g], 0.0, EPS_TOK, ALU.max, ALU.add
                                   ).then_inc(var2_ready, 1)

            def rstd_tokens(g):
                pool.wait_ge(r2_ready, g + 1)
                pool.wait_ge(var2_ready, g + 1)
                newton(norm2_l, g, var2[:, g], r2[:, g], n2, rstd2[:, g].rearrange("p b s j -> p (b s j)"),
                       rstd2_ready)

            def pair_take(q):
                pool.wait_ge(rest_ready, 2 * q + 2)
                pool.tensor_tensor(picked[:], prob[:], rest[:], ALU.subtract).then_inc(picked_ready, 1)
                pool.wait_ge(picked_ready, q + 1)
                pool.tensor_scalar(take[:, q], picked[:], rden[:, q:q + 1], 1.0, ALU.mult, ALU.mult
                                   ).then_inc(take_ready, 1)

            for k in range(STEPS):
                groups((centre_tokens, k), (var_tokens, k - 2), (rstd_tokens, k - 2), (order_input, k),
                       (rstd_input, k), (add_even_turns, k - 1), (pair_take, pair_at(k, 3)))
            pair_take(LAST)

        @block.scalar
        def _(act):
            def square_input(g):
                act.wait_ge(centred, g + 1)
                reach(act, ssum1_ready, g)
                act.activation(square1[:], y_tok[:, g % 2].rearrange("p k b c -> p (k b c)"), ACT.Square
                               ).then_inc(square1_ready, 1)

            def rsqrt_input(g):
                act.wait_ge(ssum1_ready, g + 1)
                act.activation(ln1[:, g], ssum1[:, g], ACT.Ln, bias=eps_in[:, 0:1], scale=1.0 / C
                               ).then_inc(ln1_link, 1)
                act.wait_ge(ln1_link, g + 1)
                act.activation(r1[:, g], ln1[:, g], ACT.Exp, scale=-0.5).then_inc(r1_ready, 1)

            def keep_y(g):
                act.wait_ge(y_turned, SH * g + SH)
                reach(act, conv_done, SH * (g - 1))
                act.activation(
                    y_chan[:, g % 2].rearrange("p (s k j) -> p s j k", s=SH, j=J),
                    psum[:, TURN:TURN + SH].rearrange("p s (j k) -> p s j k", j=J), ACT.Copy,
                    accum_out=chan_sum[:, g:g + 1]).then_inc(y_chan_ready, 1)

            def exp_rot(g):
                act.wait_ge(rot_nmax_ready, g + 1)
                act.activation(rot_exp[:, g], rot_logit[:, g], ACT.Exp, bias=rot_nmax[:, g:g + 1],
                               accum_out=rot_den[:, g:g + 1]).then_inc(rot_exp_ready, 1)

            def weigh_even_turns(g):
                act.wait_ge(rot_w_ready, g + 1)
                act.wait_ge(y_chan_ready, g + 1)
                reach(act, even_turns_ready, g)
                for t, i in ((turn0, 0), (turn2, 2)):
                    act.activation(t[:], y_chan[:, g % 2], ACT.Copy, scale=rot_w[:, g, i:i + 1]
                                   ).then_inc(turns_ready, 1)

            def keep_x1(g):
                for s in range(SH):
                    act.wait_ge(x1_turned, SH * g + s + 1)
                    if s == 0:
                        reach(act, ssum2_ready, g)
                    turned = psum[:, TURN + s].rearrange("p (j b c) -> p b j c", j=J, c=C)
                    act.activation(square2[:, :, s], turned, ACT.Square).then_inc(square2_ready, 1)
                    act.activation(x1[:, g * GB:g * GB + GB, s], turned, ACT.Copy).then_inc(x1_kept, 1)

            def square_means(g):
                for s in range(SH):
                    act.wait_ge(logits_done, SH * g + s + 1)
                    m = psum[:, LOGI + s, 0:J * LC].rearrange("p (j k) -> p j k", k=LC)[:, :, GB * E:LC]
                    act.activation(msq2[:, g, :, s].rearrange("p b j -> p j b"), m, ACT.Square
                                   ).then_inc(msq2_ready, 1)

            def rsqrt_tokens(g):
                act.wait_ge(var2_ready, g + 1)
                act.activation(ln2[:, g], var2[:, g], ACT.Ln).then_inc(ln2_link, 1)
                act.wait_ge(ln2_link, g + 1)
                act.activation(r2[:, g], ln2[:, g], ACT.Exp, scale=-0.5).then_inc(r2_ready, 1)

            def pair_exp(q):
                act.wait_ge(neg_max_ready, q + 1)
                reach(act, picked_ready, q)
                act.activation(prob[:].rearrange("p (s k j) -> p s j k", s=SH, j=J),
                               psum[:, ROWS:ROWS + SH].rearrange("p s (j k) -> p s j k", j=J),
                               ACT.Exp, bias=neg_max[:, q:q + 1], accum_out=den[:, q:q + 1]
                               ).then_inc(prob_ready, 1)
                act.activation(top_e[:, q], top[:, q], ACT.Exp, bias=neg_max[:, q:q + 1]
                               ).then_inc(prob_ready, 1)

            def pair_keep_slots(q):
                act.wait_ge(gathered, q + 1)
                act.activation(slots[:, q * PB:q * PB + PB].rearrange("p b e -> p (b e)"),
                               psum[0:C, ROWS, 0:PB * E], ACT.Copy).then_inc(slots_ready, 1)

            def hidden_units(w):
                lo, hi = WAVES[w]
                n = (hi - lo) * PB
                for i in range(2):
                    act.wait_ge(hidden_done, 2 * w + i + 1)
                    act.activation(hidden[:, 8 * i:8 * i + 8, lo * PB:hi * PB],
                                   psum[:, HID[w] + i, 0:8 * n].rearrange("p (e b) -> p e b", b=n), ACT.Gelu
                                   ).then_inc(hidden_ready, 1)

            act.preload_act_table_set("natural_log_exp_and_others")
            act.wait_ge(masks, 2)
            for k in range(STEPS):
                groups((keep_y, k - 1), (keep_x1, k - 2), (square_input, k), (exp_rot, k - 1),
                       (square_means, k - 2), (rsqrt_tokens, k - 2), (weigh_even_turns, k - 1),
                       (rsqrt_input, k), (pair_exp, pair_at(k, 3)), (pair_keep_slots, pair_at(k, 4)))
            pair_exp(LAST)
            hidden_units(0)
            pair_keep_slots(LAST)
            hidden_units(1)

        @block.vector
        def _(dve):
            dve.wait_ge(masks, 2)
            dve.tensor_scalar(gate_mean[:, GB * E:LC],
                              same_image[:].rearrange("p (b c) -> p c b", c=C)[:, 0], 1.0 / C, None,
                              ALU.mult).then_inc(gate_set, 1)

            gate_l = Links(dve, gate_link, 3)
            max_l = Links(dve, max_link, 2)

            def gate_rows_ready():
                dve.wait_ge(c_loaded, N_CONST)
                gate_l.begin(0)
                gate_l.then(dve.tensor_reduce(gate_sum[:], gate_rows[:], AX.X, ALU.add))
                gate_l.then(dve.tensor_scalar(gate_avg[:], gate_sum[:], 1.0 / C, None, ALU.mult))
                gate_l.then(dve.tensor_scalar(gate_cent[:], gate_rows[:], gate_avg[:, 0:1], None,
                                              ALU.subtract))
                gate_l.end()
                dve.tensor_tensor(gate_diag[:], own_slot[0:GB * E, 0:GB],
                                  gate_cent[:].unsqueeze(1).broadcast_to([GB * E, GB, C]), ALU.mult
                                  ).then_inc(gate_diag_ready, 1)

            def gate_columns():
                dve.wait_ge(gate_turned, 1)
                dve.tensor_copy(gate_mean[:, 0:GB * E], psum[:, LOGI, 0:GB * E]).then_inc(gate_ready, 1)
                dve.tensor_copy(b2[:], psum[0:O, LOGI + 1, 0:E]).then_inc(gate_ready, 1)

            def sum_input(g):
                dve.wait_ge(x_loaded[g % 2], 16 * (g // 2 + 1))
                dve.tensor_reduce(sum1[:, g], x_in[:, g % 2].rearrange("p b s (j c) -> p (b s j) c", c=C),
                                  AX.X, ALU.add).then_inc(sum1_ready, 1)

            def ssum_input(g):
                dve.wait_ge(square1_ready, g + 1)
                dve.tensor_reduce(ssum1[:, g], square1[:].rearrange("p (k c) -> p k c", c=C), AX.X, ALU.add
                                  ).then_inc(ssum1_ready, 1)

            def norm_input(g):
                dve.wait_ge(rstd1_ready, g + 1)
                y = y_tok[:, g % 2].rearrange("p k b c -> p (k b) c")
                dve.tensor_tensor(y, y, rstd1[:, g].unsqueeze(2).broadcast_to([P, GT, C]), ALU.mult
                                  ).then_inc(y_ready, 1)

            def pool_image(g):
                dve.wait_ge(y_chan_ready, g + 1)
                dve.tensor_scalar(wsel_rhs[:, g], wsel[:], chan_sum[:, g:g + 1], 1.0 / S, ALU.mult,
                                  ALU.mult).then_inc(wsel_rhs_ready, 1)

            def rot_max(g):
                dve.wait_ge(rot_logits, g + 1)
                dve.tensor_tensor(rot_logit[:, g], psum[:, LOGI, ROT_AT:ROT_AT + ROTS], bsel[:], ALU.add
                                  ).then_inc(rot_logit_ready, 1)
                dve.wait_ge(rot_logit_ready, g + 1)
                dve.tensor_reduce(rot_nmax[:, g:g + 1], rot_logit[:, g], AX.X, ALU.max, negate=True
                                  ).then_inc(rot_nmax_ready, 1)

            def rot_weights(g):
                dve.wait_ge(rot_exp_ready, g + 1)
                dve.reciprocal(rot_rden[:, g:g + 1], rot_den[:, g:g + 1]).then_inc(rot_rden_link, 1)
                dve.wait_ge(rot_rden_link, g + 1)
                dve.tensor_scalar(rot_w[:, g], rot_exp[:, g], rot_rden[:, g:g + 1], None, ALU.mult
                                  ).then_inc(rot_w_ready, 1)
                reach(dve, conv_done, SH * g)
                for i in range(2):
                    dve.tensor_scalar(diag[:, i], ident[:], rot_exp[:, g, 2 * i + 1:2 * i + 2],
                                      rot_rden[:, g:g + 1], ALU.mult, ALU.mult).then_inc(diag_ready, 1)

            def add_turns(g):
                dve.wait_ge(even_turns_ready, g + 1)
                dve.wait_ge(conv_done, SH * g + SH)
                reach(dve, logits_done, SH * (g - 1))
                dve.tensor_tensor(x1_chan[:, g % 2],
                                  psum[:, CONV:CONV + SH].rearrange("p s (j k) -> p s j k", j=J),
                                  even_turns[:].rearrange("p (s k j) -> p s j k", s=SH, j=J), ALU.add
                                  ).then_inc(x1_ready, 1)

            def ssum_tokens(g):
                dve.wait_ge(square2_ready, SH * g + SH)
                dve.tensor_reduce(ssum2[:, g], square2[:].rearrange("p b s j c -> p (b s j) c"), AX.X,
                                  ALU.add).then_inc(ssum2_ready, 1)

            def norm_logits(g):
                dve.wait_ge(rstd2_ready, g + 1)
                dve.wait_ge(logits_done, SH * g + SH)
                reach(dve, rows_done, g // 2)
                for s in range(SH):
                    dve.tensor_tensor(
                        logit_tok[:, s * J:s * J + J, g % 2],
                        psum[:, LOGI + s, 0:J * LC].rearrange("p (j k) -> p j k", k=LC)[:, :, 0:GB * E]
                        .rearrange("p j (b e) -> p j b e", e=E),
                        rstd2[:, g, :, s].rearrange("p b j -> p j b").unsqueeze(3)
                        .broadcast_to([P, J, GB, E]), ALU.mult).then_inc(logit_ready, 1)

            def pair_max(q):
                dve.wait_ge(rows_done, q + 1)
                max_l.begin(q)
                max_l.then(dve.max(top[:, q], psum[:, ROWS:ROWS + SH].rearrange("p s k -> p (s k)")))
                max_l.then(dve.tensor_tensor(gb_max[:, q:q + 1], top[:, q, 0:1], gateb[:], ALU.add))
                max_l.end()
                dve.tensor_tensor(neg_max[:, q:q + 1], gateb[:], gb_max[:, q:q + 1], ALU.subtract
                                  ).then_inc(neg_max_ready, 1)

            def pair_remove_top(q):
                dve.wait_ge(prob_ready, 2 * q + 2)
                reach(dve, picked_ready, q)
                dve.reciprocal(rden[:, q:q + 1], den[:, q:q + 1]).then_inc(rest_ready, 1)
                dve.match_replace(rest[:], top_e[:, q], prob[:], 0.0).then_inc(rest_ready, 1)

            def pair_turn_take(q):
                reach(dve, gathered, q)
                for s in range(SH):
                    dve.wait_ge(take_turned, SH * q + s + 1)
                    dve.tensor_tensor(
                        take_tok[:, s * J:s * J + J],
                        psum[:, ROWS + s].rearrange("p (j b e) -> p j b e", j=J, e=E),
                        rstd2[:, 2 * q:2 * q + 2].rearrange("p g b s j -> p s j (g b)")[:, s].unsqueeze(3)
                        .broadcast_to([P, J, PB, E]), ALU.mult).then_inc(take_tok_ready, 1)

            def centre_slots(w):
                lo, hi = WAVES[w]
                n = (hi - lo) * PB * E
                dve.wait_ge(slots_centred, w + 1)
                dve.tensor_copy(slots_c[0:C, lo * PB:hi * PB].rearrange("p b e -> p (b e)"),
                                psum[0:C, SMALL, 0:n]).then_inc(slots_c_ready, 1)

            def bias_out(w):
                lo, hi = WAVES[w]
                n = (hi - lo) * PB
                dve.wait_ge(slot_out_done, w + 1)
                dve.tensor_tensor(slot_out[:, lo * PB:hi * PB],
                                  psum[0:O, OUTS, 0:E * n].rearrange("p (e b) -> p b e", b=n),
                                  b2[:].unsqueeze(1).broadcast_to([O, n, E]), ALU.add
                                  ).then_inc(slot_out_ready, 1)

            def spread_out(w):
                lo, hi = WAVES[w]
                dve.wait_ge(slot_out_turned, w + 1)
                for q in range(lo, hi):
                    dve.tensor_tensor(spread[:, q],
                                      psum[:, SMALL, q * O:q * O + O].unsqueeze(1).broadcast_to([P, PB, O]),
                                      own_slot[:], ALU.mult).then_inc(spread_ready, 1)

            def pair_add_slots(q):
                for n in range(q * PAIR_SUMS, (q + 1) * PAIR_SUMS):
                    q, s, j, bank = final_sum(n)
                    dve.wait_ge(scattered, n + 1)
                    v = x1[:, q * PB:q * PB + PB, s, j:j + 2].rearrange("p b j c -> p j b c")
                    dve.tensor_tensor(v, psum[:, bank].rearrange("p (j b c) -> p j b c", j=2, c=O),
                                      v, ALU.add).then_inc(added, 1)

            for k in range(STEPS):
                if k == 1:
                    gate_rows_ready()
                    gate_columns()
                groups((sum_input, k), (pool_image, k - 1), (pair_max, pair_at(k, 3)),
                       (pair_turn_take, pair_at(k, 4)), (rot_max, k - 1), (ssum_tokens, k - 2),
                       (ssum_input, k), (rot_weights, k - 1), (pair_remove_top, pair_at(k, 3)),
                       (norm_logits, k - 2), (norm_input, k), (add_turns, k - 1))
            pair_max(LAST)
            centre_slots(0)
            pair_remove_top(LAST)
            bias_out(0)
            pair_turn_take(LAST)
            spread_out(0)
            pair_add_slots(0)
            centre_slots(1)
            pair_add_slots(1)
            bias_out(1)
            pair_add_slots(2)
            spread_out(1)
            pair_add_slots(LAST)

        @block.tensor
        def _(pe):
            pe.wait_ge(masks, 2)

            def gate_turn():
                pe.wait_ge(gate_diag_ready, 1)
                pe.transpose(psum[:, LOGI, 0:GB * E], gate_diag[:].rearrange("p b c -> p (b c)"),
                             ident[0:GB * E, 0:GB * E])
                pe.transpose(psum[0:O, LOGI + 1, 0:E], b2_rows[:], ident[0:E, 0:E]
                             ).then_inc(gate_turned, 1)

            def columns(t, g, k):
                return t[:, g % 2, k].rearrange("p b c -> p (b c)")

            def turn_y(g):
                pe.wait_ge(y_ready, g + 1)
                for s in range(SH):
                    reach(pe, x1_kept, SH * (g - 2) + s + 1)
                    for j in range(J):
                        mm = pe.transpose(psum[:, TURN + s, j * P:j * P + P], columns(y_tok, g, s * J + j),
                                          ident[:])
                    mm.then_inc(y_turned, 1)

            def turn_x(g):
                pe.wait_ge(x_ordered, g + 1)
                reach(pe, x1_ready, g)
                for s in range(SH):
                    for j in range(J):
                        mm = pe.matmul(psum[:, CONV + s, j * P:j * P + P], columns(x_cols, g, s * J + j),
                                       ident[:], start=(j == 0), stop=False, is_transpose=True,
                                       skip_group_check=True)
                mm.then_inc(x_turned, 1)

            def rot_select(g):
                pe.wait_ge(wsel_rhs_ready, g + 1)
                reach(pe, logit_ready, SH * (g - 1) - SH + 1)
                if g == 0:
                    pe.wait_ge(gate_ready, 2)
                pe.matmul(psum[:, LOGI, ROT_AT:ROT_AT + ROTS], same_image[:], wsel_rhs[:, g], start=True,
                          stop=True).then_inc(rot_logits, 1)

            def add_odd_turns(g):
                pe.wait_ge(diag_ready, 2 * g + 2)
                img = y_chan[:, g % 2].rearrange("p (h w) -> p h w", w=WW)
                t1 = img[:, :, ::-1].rearrange("p (v j) h -> p j h v", j=J)
                t3 = img[:, ::-1, :].rearrange("p (v j) h -> p j h v", j=J)
                hs = HH // SH
                for s in range(SH):
                    for i, t in enumerate((t1, t3)):
                        mm = pe.matmul(psum[:, CONV + s], diag[:, i], t[:, :, s * hs:s * hs + hs],
                                       start=False, stop=(i == 1), skip_group_check=True)
                    mm.then_inc(conv_done, 1)

            def turn_x1(g):
                pe.wait_ge(x1_ready, g + 1)
                pe.wait_ge(y_chan_ready, min(g + 2, NG))
                for s in range(SH):
                    for j in range(J):
                        mm = pe.transpose(psum[:, TURN + s, j * P:j * P + P], x1_chan[:, g % 2, s, j],
                                          ident[:])
                    mm.then_inc(x1_turned, 1)

            def gate_logits(g):
                pe.wait_ge(rot_logit_ready, min(g + 2, NG))
                pe.wait_ge(gate_ready, 2)
                pe.wait_ge(gate_set, 1)
                for s in range(SH):
                    reach(pe, logit_ready, SH * (g - 1) + s + 1)
                    for j in range(J):
                        mm = pe.matmul(psum[:, LOGI + s, j * LC:j * LC + LC], x1_chan[:, g % 2, s, j],
                                       gate_mean[:], start=True, stop=True)
                    mm.then_inc(logits_done, 1)

            def pair_turn_logits(q):
                pe.wait_ge(logit_ready, 2 * SH * q + 2 * SH)
                reach(pe, slots_ready, q)
                for k in range(K):
                    mm = pe.transpose(psum[:, ROWS + k // J, (k % J) * P:(k % J + 1) * P],
                                      logit_tok[:, k].rearrange("p g b e -> p (g b e)"), ident[:])
                mm.then_inc(rows_done, 1)

            def pair_turn_take(q):
                pe.wait_ge(take_ready, q + 1)
                rows = take[:, q].rearrange("p (s k j) -> p s j k", s=SH, j=J)
                for s in range(SH):
                    for j in range(J):
                        mm = pe.transpose(psum[:, ROWS + s, j * P:j * P + P], rows[:, s, j], ident[:])
                    mm.then_inc(take_turned, 1)

            def pair_gather(q):
                pe.wait_ge(take_tok_ready, SH * q + SH)
                pe.wait_ge(x1_kept, 2 * SH * q + 2 * SH)
                for b in range(PB):
                    for k in range(K):
                        mm = pe.matmul(psum[0:C, ROWS, b * E:b * E + E], x1[:, q * PB + b, k // J, k % J],
                                       take_tok[:, k, b], start=(k == 0), stop=(k == K - 1))
                mm.then_inc(gathered, 1)

            def centre_slots(w):
                lo, hi = WAVES[w]
                pe.wait_ge(slots_ready, hi)
                if w == 0:
                    pe.wait_ge(x1_kept, SH * NG)
                else:
                    pe.wait_ge(spread_ready, lo)
                pe.matmul(psum[0:C, SMALL, 0:(hi - lo) * PB * E], centre[:],
                          slots[:, lo * PB:hi * PB].rearrange("p b e -> p (b e)"), start=True, stop=True
                          ).then_inc(slots_centred, 1)

            def hidden_units(w):
                lo, hi = WAVES[w]
                n = (hi - lo) * PB
                if w == 0:
                    pe.wait_ge(x1_ready, NG)
                pe.wait_ge(w_loaded, 32)
                pe.wait_ge(slots_c_ready, w + 1)
                for e in range(E):
                    mm = pe.matmul(psum[:, HID[w] + e // 8, (e % 8) * n:(e % 8 + 1) * n], w1[:, e],
                                   slots_c[:, lo * PB:hi * PB, e], start=True, stop=True)
                    if e % 8 == 7:
                        mm.then_inc(hidden_done, 1)

            def slot_outputs(w):
                lo, hi = WAVES[w]
                n = (hi - lo) * PB
                for e in range(E):
                    if e % 8 == 0:
                        pe.wait_ge(hidden_ready, 2 * w + e // 8 + 1)
                    mm = pe.matmul(psum[0:O, OUTS, e * n:e * n + n], w2[:, e], hidden[:, e, lo * PB:hi * PB],
                                   start=True, stop=True)
                mm.then_inc(slot_out_done, 1)

            def turn_outputs(w):
                lo, hi = WAVES[w]
                pe.wait_ge(slot_out_ready, w + 1)
                for q in range(lo, hi):
                    mm = pe.transpose(psum[:, SMALL, q * O:q * O + O],
                                      slot_out[:, q * PB:q * PB + PB].rearrange("p b e -> p (b e)"),
                                      ident[0:O, 0:O])
                mm.then_inc(slot_out_turned, 1)

            def pair_scatter(q):
                pe.wait_ge(spread_ready, q + 1)
                if q == 0:
                    pe.wait_ge(logit_ready, SH * NG)
                    pe.wait_ge(hidden_ready, 2)
                for n in range(q * PAIR_SUMS, (q + 1) * PAIR_SUMS):
                    _, s, j, bank = final_sum(n)
                    rows = take[:, q].rearrange("p (s k j) -> p s j k", s=SH, j=J)
                    reach(pe, added, n - SUM_BANKS + 1)
                    for i in range(2):
                        mm = pe.matmul(psum[:, bank, i * PB * O:(i + 1) * PB * O], rows[:, s, j + i],
                                       spread[:, q].rearrange("p b o -> p (b o)"), start=True, stop=True)
                    mm.then_inc(scattered, 1)

            for k in range(STEPS):
                if k == 1:
                    gate_turn()
                groups((turn_y, k - 1), (pair_turn_logits, pair_at(k, 3)), (pair_turn_take, pair_at(k, 4)),
                       (rot_select, k - 1), (turn_x1, k - 2), (turn_x, k - 1), (gate_logits, k - 2),
                       (add_odd_turns, k - 1), (pair_gather, pair_at(k, 4)))
            pair_turn_logits(LAST)
            centre_slots(0)
            hidden_units(0)
            pair_turn_take(LAST)
            slot_outputs(0)
            turn_outputs(0)
            pair_scatter(0)
            pair_gather(LAST)
            centre_slots(1)
            pair_scatter(1)
            hidden_units(1)
            slot_outputs(1)
            pair_scatter(2)
            turn_outputs(1)
            pair_scatter(LAST)


_INS = ["x", "L0_conv_W_sel", "L0_conv_b_sel", "L0_ffn_gate_w", "L0_ffn_gate_b", "L0_ffn_weight1", "L0_ffn_weight2"]
_OUTS = [((32, 32, 32, 32), "float32")]


def kernel(**inputs):
    import numpy as _np
    import concourse.bacc as _bacc
    from concourse import mybir as _mybir
    from concourse.bass_utils import run_bass_kernel_spmd as _run

    nc = _bacc.Bacc("TRN2", target_bir_lowering=False, num_devices=1)
    arrays, args = {}, []
    for name in _INS:
        a = _np.ascontiguousarray(inputs[name])
        arrays[f"in_{name}_dram"] = a
        args.append(nc.dram_tensor(f"in_{name}_dram", a.shape, _mybir.dt.from_np(a.dtype), kind="ExternalInput").ap())
    for i, (shape, dtype) in enumerate(_OUTS):
        dt = _mybir.dt.from_np(_np.dtype(dtype))
        args.append(nc.dram_tensor(f"out_{i}_dram", shape, dt, kind="ExternalOutput").ap())
    rotate_and_route_kernel(nc, *args)
    r = _run(nc, [arrays], core_ids=[0])
    return r.results[0]["out_0_dram"]
```

```python
from contextlib import ExitStack

import concourse.bass as bass
from concourse import mybir

ALU = mybir.AluOpType
ACT = mybir.ActivationFunctionType
AX = mybir.AxisListType
F32 = mybir.dt.float32

P = 128
BANK = 512
TOPK = 8
ROTS = 4
EPS_IN = 1e-6
EPS_TOK = 1e-5


class Links:

    def __init__(self, eng, sem, per):
        self.eng, self.sem, self.per = eng, sem, per

    def begin(self, n):
        self.base, self.i = n * self.per, 0

    def then(self, ins):
        self.i += 1
        ins.then_inc(self.sem, 1)
        self.eng.wait_ge(self.sem, self.base + self.i)

    def end(self):
        assert self.i == self.per, (self.i, self.per)


def reach(eng, sem, value):
    if value > 0:
        eng.wait_ge(sem, value)


def rotate_and_route_kernel(
    nc: bass.Bass,
    x: bass.AP,
    W_sel: bass.AP,
    b_sel: bass.AP,
    gate_w: bass.AP,
    gate_b: bass.AP,
    weight1: bass.AP,
    weight2: bass.AP,
    out: bass.AP,
):
    B, HH, WW, C = x.shape
    E, _, H = weight1.shape
    O = weight2.shape[2]
    S = HH * WW
    GB = P // C
    NG = B // GB
    NP = NG // 2
    SH = S // BANK
    J = BANK // P
    K = SH * J
    GT = GB * K
    PB = 2 * GB
    RB = P // C
    LC = GB * E + GB
    WAVES = [(0, 3), (3, 4)]
    assert (HH, WW, C, E, H, O) == (32, 32, 32, 16, 128, 32) and PB * E == P and NG % 2 == 0

    with ExitStack() as ctx:
        def sb(name, shape):
            return ctx.enter_context(nc.sbuf_tensor(name, shape, F32))

        def sem(name):
            return ctx.enter_context(nc.semaphore(name))

        psum = ctx.enter_context(nc.psum_tensor("psum", [P, 8, BANK], F32))
        TURN, CONV, LOGI, ROWS = 0, 2, 4, 6
        ROT_AT = J * LC

        ident = sb("ident", [P, P])
        same_image = sb("same_image", [P, P])
        own_slot = sb("own_slot", [P, PB, O])
        eps_in = sb("eps_in", [P, 1])
        gate_rows = sb("gate_rows", [GB * E, C])
        gate_sum = sb("gate_sum", [GB * E, 1])
        gate_avg = sb("gate_avg", [GB * E, 1])
        gate_cent = sb("gate_cent", [GB * E, C])
        gate_diag = sb("gate_diag", [GB * E, GB, C])
        gate_mean = sb("gate_mean", [P, LC])
        wsel = sb("wsel", [P, ROTS])
        bsel = sb("bsel", [P, ROTS])
        gateb = sb("gateb", [P, 1])
        w1 = sb("w1", [P, E // RB, H])
        b1 = sb("b1", [E, H])
        w2 = sb("w2", [H, E, O])
        b2_rows = sb("b2_rows", [E, O])
        b2 = sb("b2", [O, E])
        centre = sb("centre", [C, RB, C])

        x_in = sb("x_in", [P, 2, GB, SH, J * C])
        x_cols = sb("x_cols", [P, 2, K, GB, C])
        y_tok = sb("y_tok", [P, 2, K, GB, C])
        square1 = sb("square1", [P, K, GB, C])
        y_chan = sb("y_chan", [P, 2, S])
        turn0 = sb("turn0", [P, S])
        turn2 = sb("turn2", [P, S])
        even_turns = sb("even_turns", [P, S])
        x1_chan = sb("x1_chan", [P, 2, SH, J, P])
        square2 = sb("square2", [P, GB, SH, J, C])

        sum1 = sb("sum1", [P, NG, GT])
        mean1 = sb("mean1", [P, NG, GT])
        ssum1 = sb("ssum1", [P, NG, GT])
        var1 = sb("var1", [P, NG, GT])
        ln1 = sb("ln1", [P, NG, GT])
        r1 = sb("r1", [P, NG, GT])
        n1 = sb("n1", [P, 2, NG, GT])
        rstd1 = sb("rstd1", [P, NG, GT])
        chan_sum = sb("chan_sum", [P, NG])
        wsel_rhs = sb("wsel_rhs", [P, NG, ROTS])
        rot_logit = sb("rot_logit", [P, NG, ROTS])
        rot_nmax = sb("rot_nmax", [P, NG])
        rot_exp = sb("rot_exp", [P, NG, ROTS])
        rot_den = sb("rot_den", [P, NG])
        rot_rden = sb("rot_rden", [P, NG])
        rot_w = sb("rot_w", [P, NG, ROTS])
        diag = sb("diag", [P, 2, P])
        ssum2 = sb("ssum2", [P, NG, GT])
        msq2 = sb("msq2", [P, NG, GB, SH, J])
        vraw2 = sb("vraw2", [P, NG, GT])
        var2 = sb("var2", [P, NG, GT])
        ln2 = sb("ln2", [P, NG, GT])
        r2 = sb("r2", [P, NG, GT])
        n2 = sb("n2", [P, 2, NG, GT])
        rstd2 = sb("rstd2", [P, NG, GB, SH, J])

        logit_tok = sb("logit_tok", [P, K, 2, GB, E])
        top = sb("top", [P, NP, TOPK])
        top_e = sb("top_e", [P, NP, TOPK])
        gb_max = sb("gb_max", [P, NP])
        neg_max = sb("neg_max", [P, NP])
        den = sb("den", [P, NP])
        rden = sb("rden", [P, NP])
        prob = sb("prob", [P, S])
        rest = sb("rest", [P, S])
        picked = sb("picked", [P, S])
        take_tok = sb("take_tok", [P, K, PB, E])

        x1 = sb("x1", [P, B, SH, J, C])
        take = sb("take", [P, NP, S])
        slots = sb("slots", [C, B, E])
        slots_c = sb("slots_c", [P, E, B])
        hidden = sb("hidden", [H, E, B])
        slot_out = sb("slot_out", [O, B, E])
        spread = sb("spread", [P, NP, PB, O])

        x_first_loaded = sem("x_first_half_loaded")
        x_loaded = [sem("x_loaded_even"), sem("x_loaded_odd")]
        c_loaded = sem("constants_loaded")
        w_loaded = sem("expert_weights_loaded")
        mask_link = sem("mask_link")
        masks = sem("masks_made")
        gate_set = sem("gate_set")
        gate_link = sem("gate_link")
        gate_diag_ready = sem("gate_diag_ready")
        gate_turned = sem("gate_turned")
        gate_ready = sem("gate_ready")
        sum1_ready = sem("sum1_ready")
        mean1_ready = sem("mean1_ready")
        x_ordered = sem("x_ordered")
        centred = sem("centred")
        square1_ready = sem("square1_ready")
        ssum1_ready = sem("ssum1_ready")
        ln1_link = sem("ln1_link")
        r1_ready = sem("r1_ready")
        var1_ready = sem("var1_ready")
        norm1_link = sem("norm1_link")
        rstd1_ready = sem("rstd1_ready")
        y_ready = sem("y_ready")
        y_turned = sem("y_turned")
        x_turned = sem("x_turned")
        y_chan_ready = sem("y_chan_ready")
        wsel_rhs_ready = sem("wsel_rhs_ready")
        rot_logits = sem("rot_logits")
        rot_logit_ready = sem("rot_logit_ready")
        rot_nmax_ready = sem("rot_nmax_ready")
        rot_exp_ready = sem("rot_exp_ready")
        rot_rden_link = sem("rot_rden_link")
        rot_w_ready = sem("rot_w_ready")
        diag_ready = sem("diag_ready")
        turns_ready = sem("turns_ready")
        even_turns_ready = sem("even_turns_ready")
        conv_done = sem("conv_done")
        x1_ready = sem("x1_ready")
        x1_turned = sem("x1_turned")
        square2_ready = sem("square2_ready")
        ssum2_ready = sem("ssum2_ready")
        msq2_ready = sem("msq2_ready")
        x1_kept = sem("x1_kept")
        logits_done = sem("logits_done")
        stat2_link = sem("stat2_link")
        var2_ready = sem("var2_ready")
        ln2_link = sem("ln2_link")
        r2_ready = sem("r2_ready")
        norm2_link = sem("norm2_link")
        rstd2_ready = sem("rstd2_ready")
        logit_ready = sem("logit_ready")
        rows_done = sem("rows_done")
        max_link = sem("max_link")
        neg_max_ready = sem("neg_max_ready")
        prob_ready = sem("prob_ready")
        rest_ready = sem("rest_ready")
        picked_ready = sem("picked_ready")
        take_ready = sem("take_ready")
        last_take_ready = sem("last_take_ready")
        take_turned = sem("take_turned")
        take_tok_ready = sem("take_tok_ready")
        gathered = sem("gathered")
        slots_ready = sem("slots_ready")
        slots_centred = sem("slots_centred")
        slots_c_ready = sem("slots_c_ready")
        hidden_done = sem("hidden_done")
        hidden_ready = sem("hidden_ready")
        slot_out_done = sem("slot_out_done")
        slot_out_ready = sem("slot_out_ready")
        slot_out_turned = sem("slot_out_turned")
        spread_ready = sem("spread_ready")
        scattered = sem("scattered")
        added = sem("added")
        stored = sem("stored")

        x_dram = x.rearrange("(g b) h w c -> g b (h w) c", b=GB).rearrange(
            "g b (s p j) c -> g p b s (j c)", p=P, j=J)
        out_dram = out.rearrange("b h w c -> b (h w) c").rearrange(
            "b (s p j) c -> p b s (j c)", p=P, j=J)

        block = ctx.enter_context(nc.Block())

        HID = (CONV, ROWS)
        OUTS, SMALL = TURN + 1, TURN

        def groups(*stages):
            for stage, n in stages:
                if 0 <= n < (NP if stage.__name__.startswith("pair_") else NG):
                    stage(n)

        def pair_at(k, lag):
            return (k - lag - 1) // 2 if (k - lag - 1) % 2 == 0 else -1

        def once(k, at):
            return 0 if k == at else -1

        PAIR_SUMS = K // 2
        SUM_BANKS = 4

        def final_sum(n):
            return n // PAIR_SUMS, n // (J // 2) % SH, 2 * (n % (J // 2)), CONV + n % SUM_BANKS

        def parts(g):
            if g == 0:
                return [(slice(0, GB // 2), 1), (slice(GB // 2, GB), 2)]
            return [(slice(0, GB), 2 * g + 2)]

        BEFORE_CENTRE = ((x1_kept, 16), (spread_ready, 3))
        BEFORE_HIDDEN = ((x1_ready, 8), (slots_ready, 4))
        BEFORE_OUTPUTS = ((slots_c_ready, 1), (slots_c_ready, 2))
        BEFORE_TURN = ((slot_out_ready, 1), (slot_out_ready, 2))

        @block.sync
        def _(sp):
            def load(g):
                reach(sp, centred, 2 * (g - 1))
                reach(sp, x_ordered, g - 1)
                if g == 0:
                    half = GB // 2
                    sp.dma_start(x_in[:, 0, 0:half], x_dram[0][:, 0:half]).then_inc(x_first_loaded, 16)
                    sp.dma_start(x_in[:, 0, half:], x_dram[0][:, half:]).then_inc(x_loaded[0], 16)
                else:
                    sp.dma_start(x_in[:, g % 2], x_dram[g]).then_inc(x_loaded[g % 2], 16)

            load(0)
            load(1)
            sp.dma_start(gate_rows[:],
                         gate_w.unsqueeze(0).broadcast_to([GB, E, C])).then_inc(c_loaded, 16)
            sp.dma_start(b2_rows[:], weight2[:, H, :]).then_inc(c_loaded, 16)
            sp.dma_start(wsel[:],
                         W_sel.unsqueeze(0).broadcast_to([GB, C, ROTS])).then_inc(c_loaded, 16)
            sp.dma_start(gateb[:],
                         gate_b.rearrange("(a e c) -> a e c", a=1, c=1).broadcast_to([PB, E, 1])
                         ).then_inc(c_loaded, 16)
            sp.dma_start(bsel[:], b_sel.rearrange("(a k) -> a k", a=1).broadcast_to([P, ROTS])
                         ).then_inc(c_loaded, 16)
            for g in range(2, NG):
                load(g)
                if g == 3:
                    by_row = weight1[:, 0:C, :].rearrange("(k r) c h -> r c k h", r=RB)
                    for r in range(RB):
                        sp.dma_start(w1[C * r:C * r + C], by_row[r]).then_inc(w_loaded, 16)
                    sp.dma_start(b1[:], weight1[:, C, :]).then_inc(w_loaded, 16)
                    sp.dma_start(w2[:], weight2[:, 0:H, :].rearrange("e h o -> h e o")
                                 ).then_inc(w_loaded, 16)

            for q in range(NP):
                for s in range(SH):
                    sp.wait_ge(added, (q * SH + s + 1) * (J // 2))
                    b = slice(q * PB, q * PB + PB)
                    sp.dma_start(out_dram[:, b, s], x1[:, b, s].rearrange("p b j c -> p b (j c)")
                                 ).then_inc(stored, 16)
            sp.wait_ge(stored, 16 * NP * SH)

        N_CONST = 16 * 5

        @block.gpsimd
        def _(pool):
            link = Links(pool, mask_link, 8)
            link.begin(0)
            link.then(pool.memset(ident[:], 0.0))
            link.then(pool.memset(same_image[:], 1.0))
            link.then(pool.memset(own_slot[:], 1.0))
            link.then(pool.memset(eps_in[:], EPS_IN))
            link.then(pool.affine_select(out=ident[:], in_=ident[:], compare_op=ALU.not_equal, fill=1.0,
                                         base=0, pattern=[[-1, P]], channel_multiplier=1))
            v = same_image[:].rearrange("p (b c) -> p b c", c=C)
            link.then(pool.affine_select(out=v, in_=v, compare_op=ALU.is_ge, fill=0.0, base=0,
                                         pattern=[[-C, GB], [0, C]], channel_multiplier=1))
            link.then(pool.affine_select(out=v, in_=v, compare_op=ALU.is_ge, fill=0.0, base=C - 1,
                                         pattern=[[C, GB], [0, C]], channel_multiplier=-1))
            link.then(pool.affine_select(out=own_slot[:], in_=own_slot[:], compare_op=ALU.is_ge, fill=0.0,
                                         base=0, pattern=[[-E, PB], [0, O]], channel_multiplier=1))
            link.end()
            pool.affine_select(out=own_slot[:], in_=own_slot[:], compare_op=ALU.is_ge, fill=0.0,
                               base=E - 1, pattern=[[E, PB], [0, O]], channel_multiplier=-1
                               ).then_inc(masks, 1)
            pool.tensor_scalar(centre[:], ident[0:C, 0:C].unsqueeze(1).broadcast_to([C, RB, C]),
                               1.0, -1.0 / C, ALU.mult, ALU.add
                               ).then_inc(masks, 1)

            def centre_tokens(g):
                for b, n in parts(g):
                    step = 1 if g == 0 else 2
                    m = mean1[:, g].rearrange("p (b k) -> p b k", b=GB)[:, b]
                    pool.wait_ge(sum1_ready, n)
                    pool.tensor_scalar(m, sum1[:, g].rearrange("p (b k) -> p b k", b=GB)[:, b], 1.0 / C, 0.0,
                                       ALU.mult, ALU.add).then_inc(mean1_ready, step)
                    pool.wait_ge(mean1_ready, n)
                    reach(pool, y_turned, SH * (g - 1))
                    pool.tensor_tensor(y_tok[:, g % 2, :, b].rearrange("p k b c -> p b k c"),
                                       x_in[:, g % 2, b].rearrange("p b s (j c) -> p b (s j) c", c=C),
                                       m.unsqueeze(3).broadcast_to([P, b.stop - b.start, K, C]), ALU.subtract
                                       ).then_inc(centred, step)

            def order_input(g):
                pool.wait_ge(sum1_ready, 2 * g + 2)
                reach(pool, x_turned, g - 1)
                pool.tensor_scalar(x_cols[:, g % 2].rearrange("p k b c -> p b k c"),
                                   x_in[:, g % 2].rearrange("p b s (j c) -> p b (s j) c", c=C),
                                   1.0, 0.0, ALU.mult, ALU.add).then_inc(x_ordered, 1)

            def add_even_turns(g):
                pool.wait_ge(turns_ready, 2 * g + 2)
                reach(pool, x1_ready, g)
                pool.tensor_tensor(even_turns[:], turn0[:], turn2[:, ::-1], ALU.add
                                   ).then_inc(even_turns_ready, 1)

            def pair_pick(q):
                if q == NP - 1:
                    return
                pool.wait_ge(rest_ready, 2 * q + 2)
                pool.tensor_tensor(picked[:], prob[:], rest[:], ALU.subtract).then_inc(picked_ready, 1)

            def pair_weigh(q):
                if q == NP - 1:
                    return
                pool.wait_ge(picked_ready, q + 1)
                pool.tensor_scalar(take[:, q], picked[:], rden[:, q:q + 1], 1.0, ALU.mult, ALU.mult
                                   ).then_inc(take_ready, 1)

            for k in range(11):
                groups((pair_weigh, pair_at(k, 5)), (add_even_turns, k - 3), (centre_tokens, k),
                       (pair_pick, pair_at(k, 4)), (order_input, k))

        @block.scalar
        def _(act):
            def square_input(g):
                for b, n in parts(g):
                    act.wait_ge(centred, n)
                    reach(act, ssum1_ready, 2 * g)
                    act.activation(square1[:, :, b], y_tok[:, g % 2, :, b], ACT.Square
                                   ).then_inc(square1_ready, 1 if g == 0 else 2)

            def rsqrt_input(g):
                act.wait_ge(ssum1_ready, 2 * g + 2)
                act.activation(ln1[:, g], ssum1[:, g], ACT.Ln, bias=eps_in[:, 0:1], scale=1.0 / C
                               ).then_inc(ln1_link, 1)
                act.activation(var1[:, g], ssum1[:, g], ACT.Identity, bias=eps_in[:, 0:1], scale=1.0 / C
                               ).then_inc(var1_ready, 1)
                act.wait_ge(ln1_link, g + 1)
                act.activation(r1[:, g], ln1[:, g], ACT.Exp, scale=-0.5).then_inc(r1_ready, 1)

            def keep_y(g):
                act.wait_ge(y_turned, SH * g + SH)
                reach(act, conv_done, SH * (g - 1))
                act.activation(
                    y_chan[:, g % 2].rearrange("p (s k j) -> p s j k", s=SH, j=J),
                    psum[:, TURN:TURN + SH].rearrange("p s (j k) -> p s j k", j=J), ACT.Copy,
                    accum_out=chan_sum[:, g:g + 1]).then_inc(y_chan_ready, 1)

            def exp_rot(g):
                act.wait_ge(rot_nmax_ready, g + 1)
                act.activation(rot_exp[:, g], rot_logit[:, g], ACT.Exp, bias=rot_nmax[:, g:g + 1],
                               accum_out=rot_den[:, g:g + 1]).then_inc(rot_exp_ready, 1)

            def turn_diagonals(g):
                act.wait_ge(rot_w_ready, g + 1)
                reach(act, conv_done, SH * g)
                for i in range(2):
                    act.activation(diag[:, i], ident[:], ACT.Copy, scale=rot_w[:, g, 2 * i + 1:2 * i + 2]
                                   ).then_inc(diag_ready, 1)

            def weigh_even_turns(g):
                act.wait_ge(rot_w_ready, g + 1)
                act.wait_ge(y_chan_ready, g + 1)
                reach(act, even_turns_ready, g)
                for t, i in ((turn0, 0), (turn2, 2)):
                    act.activation(t[:], y_chan[:, g % 2], ACT.Copy, scale=rot_w[:, g, i:i + 1]
                                   ).then_inc(turns_ready, 1)

            def keep_x1(g):
                for s in range(SH):
                    act.wait_ge(x1_turned, SH * g + s + 1)
                    if s == 0:
                        reach(act, ssum2_ready, g)
                    turned = psum[:, TURN + s].rearrange("p (j b c) -> p b j c", j=J, c=C)
                    act.activation(square2[:, :, s], turned, ACT.Square).then_inc(square2_ready, 1)
                    act.activation(x1[:, g * GB:g * GB + GB, s], turned, ACT.Copy).then_inc(x1_kept, 1)

            def square_means(g):
                for s in range(SH):
                    act.wait_ge(logits_done, SH * g + s + 1)
                    m = psum[:, LOGI + s, 0:J * LC].rearrange("p (j k) -> p j k", k=LC)[:, :, GB * E:LC]
                    act.activation(msq2[:, g, :, s].rearrange("p b j -> p j b"), m, ACT.Square
                                   ).then_inc(msq2_ready, 1)

            def rsqrt_tokens(g):
                act.wait_ge(var2_ready, g + 1)
                act.activation(ln2[:, g], var2[:, g], ACT.Ln).then_inc(ln2_link, 1)
                act.wait_ge(ln2_link, g + 1)
                act.activation(r2[:, g], ln2[:, g], ACT.Exp, scale=-0.5).then_inc(r2_ready, 1)

            def pair_exp(q):
                act.wait_ge(neg_max_ready, q + 1)
                reach(act, picked_ready, q)
                act.activation(prob[:].rearrange("p (s k j) -> p s j k", s=SH, j=J),
                               psum[:, ROWS:ROWS + SH].rearrange("p s (j k) -> p s j k", j=J),
                               ACT.Exp, bias=neg_max[:, q:q + 1], accum_out=den[:, q:q + 1]
                               ).then_inc(prob_ready, 1)
                act.activation(top_e[:, q], top[:, q], ACT.Exp, bias=neg_max[:, q:q + 1]
                               ).then_inc(prob_ready, 1)

            def pair_keep_slots(q):
                act.wait_ge(gathered, q + 1)
                act.activation(slots[:, q * PB:q * PB + PB].rearrange("p b e -> p (b e)"),
                               psum[0:C, ROWS, 0:PB * E], ACT.Copy).then_inc(slots_ready, 1)

            def hidden_units(w):
                lo, hi = WAVES[w]
                n = (hi - lo) * PB
                act.wait_ge(hidden_done, w + 1)
                act.activation(hidden[:, :, lo * PB:hi * PB],
                               psum[:, HID[w], 0:E * n].rearrange("p (e b) -> p e b", b=n), ACT.Gelu
                               ).then_inc(hidden_ready, 1)

            act.preload_act_table_set("natural_log_exp_and_others")
            act.wait_ge(masks, 2)
            for k in range(12):
                groups((pair_keep_slots, pair_at(k, 6)), (rsqrt_input, k - 1), (pair_exp, pair_at(k, 4)),
                       (exp_rot, k - 2), (square_input, k), (keep_x1, k - 3), (square_means, k - 3),
                       (turn_diagonals, k - 2), (weigh_even_turns, k - 2), (rsqrt_tokens, k - 3),
                       (keep_y, k - 1))
            hidden_units(0)
            pair_keep_slots(3)
            hidden_units(1)

        @block.vector
        def _(dve):
            gate_l = Links(dve, gate_link, 3)
            norm1_l = Links(dve, norm1_link, 2)
            norm2_l = Links(dve, norm2_link, 2)
            max_l = Links(dve, max_link, 2)

            def gate_rows_ready(_):
                dve.wait_ge(masks, 2)
                dve.tensor_scalar(gate_mean[:, GB * E:LC],
                                  same_image[:].rearrange("p (b c) -> p c b", c=C)[:, 0], 1.0 / C, None,
                                  ALU.mult).then_inc(gate_set, 1)
                dve.wait_ge(c_loaded, N_CONST)
                gate_l.begin(0)
                gate_l.then(dve.tensor_reduce(gate_sum[:], gate_rows[:], AX.X, ALU.add))
                gate_l.then(dve.tensor_scalar(gate_avg[:], gate_sum[:], 1.0 / C, None, ALU.mult))
                gate_l.then(dve.tensor_scalar(gate_cent[:], gate_rows[:], gate_avg[:, 0:1], None,
                                              ALU.subtract))
                gate_l.end()
                dve.tensor_tensor(gate_diag[:], own_slot[0:GB * E, 0:GB],
                                  gate_cent[:].unsqueeze(1).broadcast_to([GB * E, GB, C]), ALU.mult
                                  ).then_inc(gate_diag_ready, 1)

            def gate_columns(_):
                dve.wait_ge(gate_turned, 1)
                dve.tensor_copy(gate_mean[:, 0:GB * E], psum[:, LOGI, 0:GB * E]).then_inc(gate_ready, 1)
                dve.tensor_copy(b2[:], psum[0:O, LOGI + 1, 0:E]).then_inc(gate_ready, 1)

            def sum_input(g):
                for b, n in parts(g):
                    if n == 1:
                        dve.wait_ge(x_first_loaded, 16)
                    else:
                        dve.wait_ge(x_loaded[g % 2], 16 * (g // 2 + 1))
                    dve.tensor_reduce(sum1[:, g, K * b.start:K * b.stop],
                                      x_in[:, g % 2, b].rearrange("p b s (j c) -> p (b s j) c", c=C),
                                      AX.X, ALU.add).then_inc(sum1_ready, 1 if g == 0 else 2)

            def ssum_input(g):
                for b, n in parts(g):
                    dve.wait_ge(square1_ready, n)
                    dve.tensor_reduce(ssum1[:, g].rearrange("p (k b) -> p k b", b=GB)[:, :, b],
                                      square1[:, :, b], AX.X, ALU.add).then_inc(ssum1_ready, 1 if g == 0 else 2)

            def newton(link, n, v, r, tmp, out_, ready):
                link.begin(n)
                link.then(dve.tensor_tensor(tmp[:, 0, n], r, r, ALU.mult))
                link.then(dve.scalar_tensor_tensor(tmp[:, 1, n], tmp[:, 0, n], -0.5, v, ALU.mult, ALU.mult))
                link.end()
                dve.scalar_tensor_tensor(out_, tmp[:, 1, n], 1.5, r, ALU.add, ALU.mult).then_inc(ready, 1)

            def rstd_input(g):
                dve.wait_ge(r1_ready, g + 1)
                dve.wait_ge(var1_ready, g + 1)
                newton(norm1_l, g, var1[:, g], r1[:, g], n1, rstd1[:, g], rstd1_ready)

            def var_tokens(g):
                dve.wait_ge(ssum2_ready, g + 1)
                dve.wait_ge(msq2_ready, SH * g + SH)
                dve.scalar_tensor_tensor(vraw2[:, g], ssum2[:, g], 1.0 / C,
                                         msq2[:, g].rearrange("p b s j -> p (b s j)"), ALU.mult, ALU.subtract
                                         ).then_inc(stat2_link, 1)
                dve.wait_ge(stat2_link, g + 1)
                dve.tensor_scalar(var2[:, g], vraw2[:, g], 0.0, EPS_TOK, ALU.max, ALU.add
                                  ).then_inc(var2_ready, 1)

            def rstd_tokens(g):
                dve.wait_ge(r2_ready, g + 1)
                newton(norm2_l, g, var2[:, g], r2[:, g], n2, rstd2[:, g].rearrange("p b s j -> p (b s j)"),
                       rstd2_ready)

            def norm_input(g):
                dve.wait_ge(rstd1_ready, g + 1)
                y = y_tok[:, g % 2].rearrange("p k b c -> p (k b) c")
                dve.tensor_tensor(y, y, rstd1[:, g].unsqueeze(2).broadcast_to([P, GT, C]), ALU.mult
                                  ).then_inc(y_ready, 1)

            def pool_image(g):
                dve.wait_ge(y_chan_ready, g + 1)
                dve.tensor_scalar(wsel_rhs[:, g], wsel[:], chan_sum[:, g:g + 1], 1.0 / S, ALU.mult,
                                  ALU.mult).then_inc(wsel_rhs_ready, 1)

            def rot_max(g):
                dve.wait_ge(rot_logits, g + 1)
                dve.tensor_tensor(rot_logit[:, g], psum[:, LOGI, ROT_AT:ROT_AT + ROTS], bsel[:], ALU.add
                                  ).then_inc(rot_logit_ready, 1)
                dve.wait_ge(rot_logit_ready, g + 1)
                dve.tensor_reduce(rot_nmax[:, g:g + 1], rot_logit[:, g], AX.X, ALU.max, negate=True
                                  ).then_inc(rot_nmax_ready, 1)

            def rot_weights(g):
                dve.wait_ge(rot_exp_ready, g + 1)
                dve.reciprocal(rot_rden[:, g:g + 1], rot_den[:, g:g + 1]).then_inc(rot_rden_link, 1)
                dve.wait_ge(rot_rden_link, g + 1)
                dve.tensor_scalar(rot_w[:, g], rot_exp[:, g], rot_rden[:, g:g + 1], None, ALU.mult
                                  ).then_inc(rot_w_ready, 1)

            def add_turns(g):
                dve.wait_ge(even_turns_ready, g + 1)
                dve.wait_ge(conv_done, SH * g + SH)
                reach(dve, logits_done, SH * (g - 1))
                dve.tensor_tensor(x1_chan[:, g % 2],
                                  psum[:, CONV:CONV + SH].rearrange("p s (j k) -> p s j k", j=J),
                                  even_turns[:].rearrange("p (s k j) -> p s j k", s=SH, j=J), ALU.add
                                  ).then_inc(x1_ready, 1)

            def ssum_tokens(g):
                dve.wait_ge(square2_ready, SH * g + SH)
                dve.tensor_reduce(ssum2[:, g], square2[:].rearrange("p b s j c -> p (b s j) c"), AX.X,
                                  ALU.add).then_inc(ssum2_ready, 1)

            def norm_logits(g):
                dve.wait_ge(rstd2_ready, g + 1)
                dve.wait_ge(logits_done, SH * g + SH)
                reach(dve, rows_done, g // 2)
                for s in range(SH):
                    dve.tensor_tensor(
                        logit_tok[:, s * J:s * J + J, g % 2],
                        psum[:, LOGI + s, 0:J * LC].rearrange("p (j k) -> p j k", k=LC)[:, :, 0:GB * E]
                        .rearrange("p j (b e) -> p j b e", e=E),
                        rstd2[:, g, :, s].rearrange("p b j -> p j b").unsqueeze(3)
                        .broadcast_to([P, J, GB, E]), ALU.mult).then_inc(logit_ready, 1)

            def pair_max(q):
                dve.wait_ge(rows_done, q + 1)
                max_l.begin(q)
                max_l.then(dve.max(top[:, q], psum[:, ROWS:ROWS + SH].rearrange("p s k -> p (s k)")))
                max_l.then(dve.tensor_tensor(gb_max[:, q:q + 1], top[:, q, 0:1], gateb[:], ALU.add))
                max_l.end()
                dve.tensor_tensor(neg_max[:, q:q + 1], gateb[:], gb_max[:, q:q + 1], ALU.subtract
                                  ).then_inc(neg_max_ready, 1)

            def pair_remove_top(q):
                dve.wait_ge(prob_ready, 2 * q + 2)
                reach(dve, picked_ready, q)
                dve.reciprocal(rden[:, q:q + 1], den[:, q:q + 1]).then_inc(rest_ready, 1)
                dve.match_replace(rest[:], top_e[:, q], prob[:], 0.0).then_inc(rest_ready, 1)

            def last_take(_):
                q = NP - 1
                dve.wait_ge(rest_ready, 2 * q + 2)
                dve.tensor_tensor(picked[:], prob[:], rest[:], ALU.subtract).then_inc(picked_ready, 1)
                dve.wait_ge(picked_ready, q + 1)
                dve.tensor_scalar(take[:, q], picked[:], rden[:, q:q + 1], None, ALU.mult
                                  ).then_inc(last_take_ready, 1)

            def pair_turn_take(q):
                reach(dve, gathered, q)
                for s in range(SH):
                    dve.wait_ge(take_turned, SH * q + s + 1)
                    dve.tensor_tensor(
                        take_tok[:, s * J:s * J + J],
                        psum[:, ROWS + s].rearrange("p (j b e) -> p j b e", j=J, e=E),
                        rstd2[:, 2 * q:2 * q + 2].rearrange("p g b s j -> p s j (g b)")[:, s].unsqueeze(3)
                        .broadcast_to([P, J, PB, E]), ALU.mult).then_inc(take_tok_ready, 1)

            def centre_slots(w):
                lo, hi = WAVES[w]
                n = (hi - lo) * PB
                dve.wait_ge(slots_centred, w + 1)
                dve.tensor_tensor(slots_c[:, :, lo * PB:hi * PB].rearrange("p (k r) b -> p k r b", r=RB),
                                  psum[:, SMALL, 0:n * E].rearrange("p (b k r) -> p k r b", r=RB, b=n),
                                  same_image[:].rearrange("p (r c) -> p c r", c=C)[:, 0].unsqueeze(1)
                                  .unsqueeze(3).broadcast_to([P, E // RB, RB, n]), ALU.mult
                                  ).then_inc(slots_c_ready, 1)

            def bias_out(w):
                lo, hi = WAVES[w]
                n = (hi - lo) * PB
                dve.wait_ge(slot_out_done, w + 1)
                dve.tensor_tensor(slot_out[:, lo * PB:hi * PB],
                                  psum[0:O, OUTS, 0:E * n].rearrange("p (e b) -> p b e", b=n),
                                  b2[:].unsqueeze(1).broadcast_to([O, n, E]), ALU.add
                                  ).then_inc(slot_out_ready, 1)

            def spread_out(w):
                lo, hi = WAVES[w]
                dve.wait_ge(slot_out_turned, w + 1)
                for q in range(lo, hi):
                    dve.tensor_tensor(spread[:, q],
                                      psum[:, SMALL, q * O:q * O + O].unsqueeze(1).broadcast_to([P, PB, O]),
                                      own_slot[:], ALU.mult).then_inc(spread_ready, 1)

            def pair_add_slots(q):
                for n in range(q * PAIR_SUMS, (q + 1) * PAIR_SUMS):
                    q, s, j, bank = final_sum(n)
                    dve.wait_ge(scattered, n + 1)
                    v = x1[:, q * PB:q * PB + PB, s, j:j + 2].rearrange("p b j c -> p j b c")
                    dve.tensor_tensor(v, psum[:, bank].rearrange("p (j b c) -> p j b c", j=2, c=O),
                                      v, ALU.add).then_inc(added, 1)

            for k in range(11):
                groups((rot_weights, k - 3), (gate_columns, once(k, 2)), (sum_input, k),
                       (ssum_tokens, k - 4), (var_tokens, k - 4), (ssum_input, k - 1),
                       (rstd_tokens, k - 4), (norm_logits, k - 4), (pool_image, k - 2),
                       (add_turns, k - 3), (gate_rows_ready, once(k, 1)), (pair_max, pair_at(k, 4)),
                       (rot_max, k - 2), (rstd_input, k - 1),
                       (pair_remove_top, pair_at(k, 4)), (pair_turn_take, pair_at(k, 5)),
                       (norm_input, k - 1))
            ssum_tokens(7)
            var_tokens(7)
            rstd_tokens(7)
            norm_logits(7)
            pair_max(3)
            centre_slots(0)
            pair_remove_top(3)
            last_take(0)
            pair_turn_take(3)
            bias_out(0)
            spread_out(0)
            pair_add_slots(0)
            centre_slots(1)
            pair_add_slots(1)
            bias_out(1)
            spread_out(1)
            pair_add_slots(2)
            pair_add_slots(3)

        @block.tensor
        def _(pe):
            pe.wait_ge(masks, 2)

            def gate_turn(_):
                pe.wait_ge(gate_diag_ready, 1)
                pe.transpose(psum[:, LOGI, 0:GB * E], gate_diag[:].rearrange("p b c -> p (b c)"),
                             ident[0:GB * E, 0:GB * E])
                pe.transpose(psum[0:O, LOGI + 1, 0:E], b2_rows[:], ident[0:E, 0:E]
                             ).then_inc(gate_turned, 1)

            def columns(t, g, k):
                return t[:, g % 2, k].rearrange("p b c -> p (b c)")

            def turn_y(g):
                pe.wait_ge(y_ready, g + 1)
                reach(pe, y_chan_ready, g)
                for s in range(SH):
                    reach(pe, x1_kept, SH * (g - 2) + s + 1)
                    for j in range(J):
                        mm = pe.transpose(psum[:, TURN + s, j * P:j * P + P], columns(y_tok, g, s * J + j),
                                          ident[:])
                    mm.then_inc(y_turned, 1)

            def turn_x(g):
                pe.wait_ge(x_ordered, g + 1)
                reach(pe, x1_ready, g)
                for s in range(SH):
                    for j in range(J):
                        mm = pe.matmul(psum[:, CONV + s, j * P:j * P + P], columns(x_cols, g, s * J + j),
                                       ident[:], start=(j == 0), stop=False, is_transpose=True,
                                       skip_group_check=True)
                mm.then_inc(x_turned, 1)

            def rot_select(g):
                pe.wait_ge(wsel_rhs_ready, g + 1)
                reach(pe, logit_ready, SH * (g - 2) + 1)
                if g == 0:
                    pe.wait_ge(gate_ready, 2)
                pe.matmul(psum[:, LOGI, ROT_AT:ROT_AT + ROTS], same_image[:], wsel_rhs[:, g], start=True,
                          stop=True).then_inc(rot_logits, 1)

            def add_odd_turns(g):
                pe.wait_ge(diag_ready, 2 * g + 2)
                img = y_chan[:, g % 2].rearrange("p (h w) -> p h w", w=WW)
                t1 = img[:, :, ::-1].rearrange("p (v j) h -> p j h v", j=J)
                t3 = img[:, ::-1, :].rearrange("p (v j) h -> p j h v", j=J)
                hs = HH // SH
                for s in range(SH):
                    for i, t in enumerate((t1, t3)):
                        mm = pe.matmul(psum[:, CONV + s], diag[:, i], t[:, :, s * hs:s * hs + hs],
                                       start=False, stop=(i == 1), skip_group_check=True)
                    mm.then_inc(conv_done, 1)

            def turn_x1(g):
                pe.wait_ge(x1_ready, g + 1)
                pe.wait_ge(y_chan_ready, min(g + 2, NG))
                for s in range(SH):
                    reach(pe, x1_kept, SH * (g - 1) + s + 1)
                    for j in range(J):
                        mm = pe.transpose(psum[:, TURN + s, j * P:j * P + P], x1_chan[:, g % 2, s, j],
                                          ident[:])
                    mm.then_inc(x1_turned, 1)

            def gate_logits(g):
                pe.wait_ge(rot_logit_ready, min(g + 2, NG))
                pe.wait_ge(gate_ready, 2)
                pe.wait_ge(gate_set, 1)
                for s in range(SH):
                    reach(pe, logit_ready, SH * (g - 1) + s + 1)
                    for j in range(J):
                        mm = pe.matmul(psum[:, LOGI + s, j * LC:j * LC + LC], x1_chan[:, g % 2, s, j],
                                       gate_mean[:], start=True, stop=True)
                    mm.then_inc(logits_done, 1)

            def pair_turn_logits(q):
                pe.wait_ge(logit_ready, 2 * SH * q + 2 * SH)
                reach(pe, slots_ready, q)
                for k in range(K):
                    mm = pe.transpose(psum[:, ROWS + k // J, (k % J) * P:(k % J + 1) * P],
                                      logit_tok[:, k].rearrange("p g b e -> p (g b e)"), ident[:])
                mm.then_inc(rows_done, 1)

            def pair_turn_take(q):
                if q < NP - 1:
                    pe.wait_ge(take_ready, q + 1)
                else:
                    pe.wait_ge(last_take_ready, 1)
                rows = take[:, q].rearrange("p (s k j) -> p s j k", s=SH, j=J)
                for s in range(SH):
                    for j in range(J):
                        mm = pe.transpose(psum[:, ROWS + s, j * P:j * P + P], rows[:, s, j], ident[:])
                    mm.then_inc(take_turned, 1)

            def pair_gather(q):
                pe.wait_ge(take_tok_ready, SH * q + SH)
                pe.wait_ge(x1_kept, 2 * SH * q + 2 * SH)
                for b in range(PB):
                    for k in range(K):
                        mm = pe.matmul(psum[0:C, ROWS, b * E:b * E + E], x1[:, q * PB + b, k // J, k % J],
                                       take_tok[:, k, b], start=(k == 0), stop=(k == K - 1))
                mm.then_inc(gathered, 1)

            def centre_slots(w):
                lo, hi = WAVES[w]
                pe.wait_ge(slots_ready, hi)
                pe.wait_ge(*BEFORE_CENTRE[w])
                pe.matmul(psum[:, SMALL, 0:(hi - lo) * PB * E], centre[:].rearrange("p r c -> p (r c)"),
                          slots[:, lo * PB:hi * PB].rearrange("p b e -> p (b e)"), start=True, stop=True
                          ).then_inc(slots_centred, 1)

            def hidden_units(w):
                lo, hi = WAVES[w]
                n = (hi - lo) * PB
                pe.wait_ge(*BEFORE_HIDDEN[w])
                pe.wait_ge(w_loaded, 16 * (RB + 2))
                pe.wait_ge(slots_c_ready, w + 1)
                pe.matmul(psum[:, HID[w], 0:E * n], b1[:], ident[0:E, 0:E].unsqueeze(2).broadcast_to([E, E, n]),
                          start=True, stop=False, skip_group_check=True)
                for k in range(E // RB):
                    mm = pe.matmul(psum[:, HID[w], k * RB * n:(k + 1) * RB * n], w1[:, k],
                                   slots_c[:, k * RB:(k + 1) * RB, lo * PB:hi * PB],
                                   start=False, stop=(k == E // RB - 1), skip_group_check=True)
                mm.then_inc(hidden_done, 1)

            def slot_outputs(w):
                lo, hi = WAVES[w]
                n = (hi - lo) * PB
                pe.wait_ge(*BEFORE_OUTPUTS[w])
                pe.wait_ge(hidden_ready, w + 1)
                for e in range(E):
                    mm = pe.matmul(psum[0:O, OUTS, e * n:e * n + n], w2[:, e], hidden[:, e, lo * PB:hi * PB],
                                   start=True, stop=True)
                mm.then_inc(slot_out_done, 1)

            def turn_outputs(w):
                lo, hi = WAVES[w]
                pe.wait_ge(slot_out_ready, w + 1)
                pe.wait_ge(*BEFORE_TURN[w])
                for q in range(lo, hi):
                    mm = pe.transpose(psum[:, SMALL, q * O:q * O + O],
                                      slot_out[:, q * PB:q * PB + PB].rearrange("p b e -> p (b e)"),
                                      ident[0:O, 0:O])
                mm.then_inc(slot_out_turned, 1)

            def pair_scatter(q):
                pe.wait_ge(spread_ready, q + 1)
                if q == 0:
                    pe.wait_ge(x1_ready, NG)
                    pe.wait_ge(logit_ready, SH * NG)
                    pe.wait_ge(hidden_ready, 1)
                for n in range(q * PAIR_SUMS, (q + 1) * PAIR_SUMS):
                    _, s, j, bank = final_sum(n)
                    rows = take[:, q].rearrange("p (s k j) -> p s j k", s=SH, j=J)
                    reach(pe, added, n - SUM_BANKS + 1)
                    for i in range(2):
                        mm = pe.matmul(psum[:, bank, i * PB * O:(i + 1) * PB * O], rows[:, s, j + i],
                                       spread[:, q].rearrange("p b o -> p (b o)"), start=True, stop=True)
                    mm.then_inc(scattered, 1)

            def keep_warm(n):
                for _ in range(n):
                    pe.matmul(psum[:, CONV + 1], ident[:], y_chan[:, 0, 0:BANK], start=True, stop=True)

            for k in range(10):
                groups((gate_turn, once(k, 0)), (pair_turn_take, pair_at(k, 4)), (rot_select, k - 1),
                       (turn_x1, k - 2), (gate_logits, k - 2), (turn_x, k - 1),
                       (pair_gather, pair_at(k, 4)), (turn_y, k), (add_odd_turns, k - 1),
                       (pair_turn_logits, pair_at(k, 2)))
            centre_slots(0)
            keep_warm(2)
            hidden_units(0)
            keep_warm(2)
            pair_turn_take(3)
            slot_outputs(0)
            pair_gather(3)
            turn_outputs(0)
            pair_scatter(0)
            centre_slots(1)
            hidden_units(1)
            pair_scatter(1)
            slot_outputs(1)
            turn_outputs(1)
            pair_scatter(2)
            pair_scatter(3)


_INS = ["x", "L0_conv_W_sel", "L0_conv_b_sel", "L0_ffn_gate_w", "L0_ffn_gate_b", "L0_ffn_weight1", "L0_ffn_weight2"]
_OUTS = [((32, 32, 32, 32), "float32")]


def kernel(**inputs):
    import numpy as _np
    import concourse.bacc as _bacc
    from concourse import mybir as _mybir
    from concourse.bass_utils import run_bass_kernel_spmd as _run

    nc = _bacc.Bacc("TRN2", target_bir_lowering=False, num_devices=1)
    arrays, args = {}, []
    for name in _INS:
        a = _np.ascontiguousarray(inputs[name])
        arrays[f"in_{name}_dram"] = a
        args.append(nc.dram_tensor(f"in_{name}_dram", a.shape, _mybir.dt.from_np(a.dtype), kind="ExternalInput").ap())
    for i, (shape, dtype) in enumerate(_OUTS):
        dt = _mybir.dt.from_np(_np.dtype(dtype))
        args.append(nc.dram_tensor(f"out_{i}_dram", shape, dt, kind="ExternalOutput").ap())
    rotate_and_route_kernel(nc, *args)
    r = _run(nc, [arrays], core_ids=[0])
    return r.results[0]["out_0_dram"]
```
